# Optimizing a Trainium2 kernel written in Bass

```python
import numpy as np
import jax
import jax.numpy as jnp

def _softmax(x, axis=-1):
    return jax.nn.softmax(x, axis=axis)

def _gelu(x):
    return jax.nn.gelu(x, approximate=True)

def _silu(x):
    return jax.nn.silu(x)

def _sigmoid(x):
    return jax.nn.sigmoid(x)

def _layernorm(x, axis=-1, eps=1e-05):
    m = jnp.mean(x, axis=axis, keepdims=True)
    v = jnp.var(x, axis=axis, keepdims=True)
    return (x - m) / jnp.sqrt(v + eps)

def _scatter_add(tgt, idx, src, axis=0):
    return tgt.at[idx].add(src)

def _segment_sum(src, seg, n):
    return jax.ops.segment_sum(src, seg, n)
kernel_name = 'mk_prb_d1_jaxref_r4_e87aea'

def setup_inputs(seed: int=0):
    np.random.seed(seed)
    _w = jnp.asarray

    def _L0_attn_setup():
        import jax, jax.numpy as jnp
        import numpy as np
        B, S, D = (2, 512, 256)
        H = 16
        DK = 256
        DV = 256
        EPS = 1e-05
        key = jax.random.key(seed)
        k1, k2, k3, k4 = jax.random.split(key, 4)
        x = jax.random.normal(k1, (B, S, D), dtype=jnp.float32)
        Wq = jax.random.normal(k2, (DK, D), dtype=jnp.float32) * 0.02
        Wk = jax.random.normal(k3, (DK, D), dtype=jnp.float32) * 0.02
        Wv = jax.random.normal(k4, (DV, D), dtype=jnp.float32) * 0.02
        return {'x': x, 'Wq': Wq, 'Wk': Wk, 'Wv': Wv}
    _L0_attn_in = _L0_attn_setup()

    def _L0_ffn_setup():
        import jax, jax.numpy as jnp
        import numpy as np
        D_MODEL = 256
        HIDDEN = 1024
        NUM_EXPERTS = 8
        TOP_K = 2
        key = jax.random.key(seed)
        k_x, k_g, k_in, k_out = jax.random.split(key, 4)
        bound_in = 1.0 / HIDDEN
        bound_out = 1.0 / D_MODEL
        x = jax.random.normal(k_x, (2, 512, D_MODEL), dtype=jnp.float32)
        w_gate = jax.random.uniform(k_g, (NUM_EXPERTS, D_MODEL), dtype=jnp.float32, minval=-D_MODEL ** (-0.5), maxval=D_MODEL ** (-0.5))
        w_in = jax.random.uniform(k_in, (NUM_EXPERTS, HIDDEN, D_MODEL), dtype=jnp.float32, minval=-bound_in, maxval=bound_in)
        w_out = jax.random.uniform(k_out, (NUM_EXPERTS, D_MODEL, HIDDEN), dtype=jnp.float32, minval=-bound_out, maxval=bound_out)
        return {'x': x, 'w_gate': w_gate, 'w_in': w_in, 'w_out': w_out}
    _L0_ffn_in = _L0_ffn_setup()
    _d = {'L0_attn_x': _L0_attn_in['x'], 'L0_attn_Wq': _L0_attn_in['Wq'], 'L0_attn_Wk': _L0_attn_in['Wk'], 'L0_attn_Wv': _L0_attn_in['Wv'], 'L0_ffn_w_gate': _L0_ffn_in['w_gate'], 'L0_ffn_w_in': _L0_ffn_in['w_in'], 'L0_ffn_w_out': _L0_ffn_in['w_out']}
    _x0 = _d['L0_attn_x']
    _d['L0_attn_x'] = jax.random.normal(jax.random.fold_in(jax.random.key(seed), 1), (4, 1024, 256), dtype=_x0.dtype)
    del _x0
    return _d

def reference(L0_attn_x, L0_attn_Wq, L0_attn_Wk, L0_attn_Wv, L0_ffn_w_gate, L0_ffn_w_in, L0_ffn_w_out):

    def _L0_attn_ref(x, Wq, Wk, Wv):
        import jax, jax.numpy as jnp
        import numpy as np
        B, S, D = (2, 512, 256)
        H = 16
        DK = 256
        DV = 256
        EPS = 1e-05
        b, s, d = x.shape
        dkh = DK // H
        dvh = DV // H
        Q = (x @ Wq.T).reshape(H, b, s, dkh)
        K = (x @ Wk.T).reshape(H, b, s, dkh)
        V = (x @ Wv.T).reshape(H, b, s, dvh)
        scores = jnp.einsum('hbqd,hbkd->hbqk', Q, K)
        atten = jax.nn.softmax(scores, axis=-1)
        out = jnp.einsum('hbqk,hbkd->hbqd', atten, V).reshape(b, s, -1)
        y = out + x
        mu = jnp.mean(y, axis=(1, 2), keepdims=True)
        var = jnp.var(y, axis=(1, 2), keepdims=True)
        return (y - mu) / jnp.sqrt(var + EPS)

    def _L0_ffn_ref(x, w_gate, w_in, w_out):
        import jax, jax.numpy as jnp
        import numpy as np
        D_MODEL = 256
        HIDDEN = 1024
        NUM_EXPERTS = 8
        TOP_K = 2
        B, S, D = x.shape
        E = w_in.shape[0]
        xt = x.reshape(-1, D)
        logits = (xt @ w_gate.T).astype(jnp.float32)
        top_logits, top_idx = jax.lax.top_k(logits, TOP_K)
        top_gates = jax.nn.softmax(top_logits, axis=-1).astype(x.dtype)
        gates = (jax.nn.one_hot(top_idx, E, dtype=x.dtype) * top_gates[..., None]).sum(axis=1)
        y = jnp.zeros_like(xt)
        for e in range(E):
            h = xt @ w_in[e].T
            y = y + gates[:, e:e + 1] * (h @ w_out[e].T)
        return y.reshape(B, S, D)
    x = L0_attn_x
    xn = _layernorm(x, axis=-1)
    x = x + _L0_attn_ref(xn, L0_attn_Wq, L0_attn_Wk, L0_attn_Wv) + _L0_ffn_ref(xn, L0_ffn_w_gate, L0_ffn_w_in, L0_ffn_w_out)
    return x

_drawn_inputs = setup_inputs


def setup_inputs(seed=0):
    import zlib

    import numpy as np

    out = dict(_drawn_inputs(seed))
    spreads = {}
    factors = {'L0_attn_Wq': 8.0,
     'L0_attn_Wk': 8.0,
     'L0_attn_Wv': 8.0,
     'L0_ffn_w_gate': 22.411,
     'L0_ffn_w_in': 8.0,
     'L0_ffn_w_out': 8.0}
    for name, (base, spread) in spreads.items():
        noise = np.random.default_rng([zlib.crc32(name.encode()), seed]).standard_normal(out[name].shape)
        drawn = base * np.exp(spread * noise) if base else spread * noise
        out[name] = jnp.asarray(drawn.astype(out[name].dtype))
    for name, factor in factors.items():
        out[name] = (out[name] * factor).astype(out[name].dtype)
    return out
```

```python
import concourse.bass as bass
from concourse import mybir
from contextlib import ExitStack


FP32 = mybir.dt.float32
BF16 = mybir.dt.bfloat16
ALU = mybir.AluOpType
ACT = mybir.ActivationFunctionType
AX = mybir.AxisListType

P = 128
EPS = 1e-5
BIG = 3e38


def attention_and_experts(nc, x, wq_t, wk_t, wv_t, wg_t, w_in, w_out_t, out):
    BATCH, S, D = x.shape
    T = BATCH * S
    NT = T // P
    KT = D // P
    HEADS = 16
    DH = D // HEADS
    NB = HEADS * BATCH
    TB = T // NB
    G = D // DH
    POS = TB * G
    NKT = POS // P
    HALF = POS // 2
    TC = 4
    CH = TC * P
    NC = T // CH
    BC = CH // TB
    E, HID, _ = w_in.shape
    HU = HID // 2 // P
    VW = DH + 1
    TERMS_Q = (0, 1, 2, 0, 1, 0)
    TERMS_K = (0, 0, 0, 1, 1, 2)
    FR = DH * len(TERMS_Q)
    SR = FR + 3
    SLOTS = 4
    TPB = NT // BATCH

    x_v = x.rearrange("a (t p) d -> p (a t) d", p=P)
    out_v = out.rearrange("a (t p) d -> p (a t) d", p=P)

    qk_d = nc.dram_tensor("qk_d", [2, KT * P, T], FP32, kind="Internal").ap()
    third_d = nc.dram_tensor("third_d", [2, 3, NB * DH, POS], BF16, kind="Internal").ap()
    xt_d = nc.dram_tensor("xt_d", [KT, P, T], FP32, kind="Internal").ap()
    max_d = nc.dram_tensor("max_d", [2, P, 32], BF16, kind="Internal").ap()

    ctx = ExitStack()
    with ctx:
        def sb(name, shape, dt=FP32):
            return ctx.enter_context(nc.sbuf_tensor(name, shape, dt))

        def sem(name, n=None):
            if n is None:
                return ctx.enter_context(nc.semaphore(name))
            return [ctx.enter_context(nc.semaphore(f"{name}{i}")) for i in range(n)]

        acc = sb("acc", [P, NT, D])
        xn = sb("xn", [P, NT, D])
        v_all = sb("v_all", [P, NB, NKT, VW])
        mt = sb("mt", [P, KT, E, D])
        wqk = sb("wqk", [P, 2, KT, D])
        wv = sb("wv", [P, KT, D])
        wg = sb("wg", [P, KT, E])
        ident = sb("ident", [P, P])
        onesm = sb("onesm", [P, P])
        xnc = sb("xnc", [P, 2, TC, D])
        xtc = sb("xtc", [P, 2, KT, CH])
        stage = sb("stage", [P, 2 * KT, CH])
        st = sb("st", [P, TC, 6])
        part = sb("part", [P, 4, TC])
        mean = sb("mean", [P, TC])
        var = sb("var", [P, TC])
        veps = sb("veps", [P, TC])
        rstd = sb("rstd", [P, TC])
        mhalf = sb("mhalf", [P, 8])
        epst = sb("epst", [P, 8])
        zero = sb("zero", [P, 8])
        lg = sb("lg", [P, NT, E])
        rank = sb("rank", [P, E])
        eq = sb("eq", [P, NT, E])
        oh1 = sb("oh1", [P, NT, E])
        oh2 = sb("oh2", [P, NT, E])
        lm = sb("lm", [P, NT, E])
        gates = sb("gates", [P, NT, E])
        top1 = sb("top1", [P, NT])
        top2 = sb("top2", [P, NT])
        first = sb("first", [P, NT])
        gap = sb("gap", [P, NT])
        ex = sb("ex", [P, NT])
        gs = sb("gs", [P, NT])
        g1 = sb("g1", [P, NT])
        g2 = sb("g2", [P, NT])
        dq = [stage[:, 2 * f:2 * f + 2, :].rearrange("p k t -> p (k t)") for f in range(2)]
        third = sb("third", [P, 2, 3, POS], BF16)
        xtt = sb("xtt", [P, 2, KT, P])
        wp = sb("wp", [P, 4, POS])
        win = [wp[:, 2 * s, :].rearrange("p (h d) -> p h d", h=HU) for s in range(2)]
        wout = [wp[:, 2 * s + 1, :].rearrange("p (h d) -> p h d", h=HU) for s in range(2)]
        qf = sb("qf", [SR, SLOTS, POS], BF16)
        kf = sb("kf", [SR, SLOTS, POS], BF16)
        vb = sb("vb", [P, 2, NKT, VW])
        negm = sb("negm", [P, 2, NKT])
        mrest = sb("mrest", [P, 2, NKT])
        mpart = sb("mpart", [P, 2, 32], BF16)
        mt32 = sb("mt32", [P, 2, 32], BF16)
        ot = sb("ot", [P, 4, 2, TB])
        rden = sb("rden", [P, 4, 4])
        att = sb("att", [P, D])
        ystat = sb("ystat", [P, NT, 6])
        bmv = sb("bmv", [P, BATCH, 2])
        dev2 = sb("dev2", [P, BATCH])
        bmean = sb("bmean", [P, BATCH, 2])
        bvar = sb("bvar", [P, BATCH])
        brstd = sb("brstd", [P, BATCH])
        bshift = sb("bshift", [P, BATCH])

        ps = ctx.enter_context(nc.psum_tensor("ps", [P, 8, 512], FP32))
        XT_BANK = (0, 1)
        QK_BANK = (2, 3, 4, 2)
        V_BANK = (5, 6)
        G_BANK = 7
        MAX_BANK = (0, 2)
        ST_BANK = (4, 5)
        PV_BANK = 6
        TR_BANK = 7

        w_small = sem("w_small")
        x_in = sem("x_in", 2)
        const_step = sem("const_step")
        stats_done = sem("stats_done")
        part_done = sem("part_done")
        mv_done = sem("mv_done")
        veps_done = sem("veps_done")
        rstd_done = sem("rstd_done")
        xn_done = sem("xn_done")
        xn_saved = sem("xn_saved", 2)
        xt_psum = sem("xt_psum", 2)
        xt_evac = sem("xt_evac")
        xt_stored = sem("xt_stored", 2)
        qk_ready = sem("qk_ready")
        qk_evac = sem("qk_evac")
        stage_out = sem("stage_out")
        v_ready = sem("v_ready")
        v_evac = sem("v_evac")
        ones_done = sem("ones_done")
        lg_ready = sem("lg_ready", 2)
        lg_evac = sem("lg_evac")
        gate_step = sem("gate_step")
        gap_done = sem("gap_done")
        gexp_done = sem("gexp_done")
        gates_done = sem("gates_done")
        dq_in = sem("dq_in", 2)
        hi_done = sem("hi_done", 2)
        r1_done = sem("r1_done", 2)
        mid_done = sem("mid_done", 2)
        lo_done = sem("lo_done", 2)
        third_out = sem("third_out", 2)
        w_in_s = sem("w_in_s", 2)
        first_half = sem("first_half")
        m_ready = sem("m_ready", 2)
        m_evac = sem("m_evac")
        xtt_in = sem("xtt_in", 2)
        y_ready = sem("y_ready", 2)
        ff_step = sem("ff_step", 2)
        att_const = sem("att_const")
        feat_in = sem("feat_in", SLOTS)
        vb_in = sem("vb_in", 2)
        st_ready = sem("st_ready", 2)
        exp_done = sem("exp_done", 2)
        pv_done = sem("pv_done", 4)
        pv_evac = sem("pv_evac")
        max_ready = sem("max_ready", 2)
        max_done = sem("max_done", 2)
        msplit = sem("msplit")
        mt_done = sem("mt_done")
        mrow_out = sem("mrow_out", 2)
        mrow_in = sem("mrow_in", SLOTS)
        tr_done = sem("tr_done")
        rden_done = sem("rden_done")
        norm_done = sem("norm_done")
        y_done = sem("y_done")
        ystat_done = sem("ystat_done")
        fin_d = sem("fin_d")
        fin_pe = sem("fin_pe")
        fin_pool = sem("fin_pool")
        z_done = sem("z_done")
        o_done = sem("o_done")
        o_out = sem("o_out", 2)

        block = ctx.enter_context(nc.Block())

        @block.sync
        def _(sp):
            with sp.Fori(0, NC // 2) as k:
                for p in range(2):
                    sp.wait_ge(x_in[p], 16 * k)
                    sp.dma_start(acc[:, bass.ds(TC * (2 * k + p), TC), :],
                                 x_v[:, bass.ds(TC * (2 * k + p), TC), :]).then_inc(x_in[p], 16)
            with sp.Fori(0, E) as e:
                for s in range(2):
                    if s == 0:
                        sp.wait_ge(first_half, e)
                    else:
                        sp.wait_ge(m_evac, KT * e)
                    rows = bass.ds(e * HID + s * HU * P, HU * P)
                    sp.dma_start(win[s], w_in.rearrange("e h d -> (e h) d")[rows, :]
                                 .rearrange("(p h) d -> p h d", h=HU)).then_inc(w_in_s[s], 16)
                    sp.dma_start(wout[s], w_out_t.rearrange("e h d -> (e h) d")[rows, :]
                                 .rearrange("(p h) d -> p h d", h=HU)).then_inc(w_in_s[s], 16)
            for p in range(2):
                sp.wait_ge(xt_stored[p], 16 * NC // 2)
            with sp.Fori(0, NT // 2) as k:
                for p in range(2):
                    sp.wait_ge(y_ready[p], 4 * k)
                    sp.dma_start(xtt[:, p], xt_d[:, :, bass.ds((2 * k + p) * P, P)]
                                 .rearrange("k p t -> p k t")).then_inc(xtt_in[p], 16)

            def features(n, slot):
                for f, (dst, terms) in enumerate(((qf, TERMS_Q), (kf, TERMS_K))):
                    for r, term in enumerate(terms):
                        sp.dma_start(dst[r * DH:(r + 1) * DH, slot, :],
                                     third_d[f, term, bass.ds(n * DH, DH), :]).then_inc(feat_in[slot], 16)

            def values(n, par):
                sp.dma_start(vb[:, par], v_all[:, bass.ds(n, 1)].rearrange("p b k v -> p (b k) v")
                             ).then_inc(vb_in[par], 16)

            def max_rows(slot, par, nth, gen_in, gen_slot):
                sp.wait_ge(mt_done, nth + 1)
                sp.wait_ge(mrow_in[(slot + 2) % SLOTS], 16 * gen_in)
                sp.dma_start(max_d[par], mt32[:, par]).then_inc(mrow_out[par], 16)
                sp.wait_ge(mrow_out[par], 16 * (gen_slot + 1))
                for c in range(3):
                    sp.dma_start(qf[FR + c:FR + c + 1, slot, :].rearrange("o (t q r) -> o t q r", q=4, r=32),
                                 max_d[par].rearrange("(q c t) r -> c t q r", q=4, c=4)[c:c + 1]
                                 ).then_inc(mrow_in[slot], 16)

            for f in range(2):
                sp.wait_ge(third_out[f], 48 * NC)
            for n in range(SLOTS):
                features(n, n)
            sp.wait_ge(v_evac, 2 * NC)
            sp.wait_ge(ones_done, 1)
            values(0, 0)
            max_rows(0, 0, 0, 0, 0)

            def step(i, u):
                n = SLOTS * i + u
                sp.wait_ge(pv_done[3], 2 * n)
                values(n + 1, (u + 1) % 2)
                m = u + 1
                max_rows(m % SLOTS, m % 2, n + 1, 3 * (i if u == 0 else i + (m - 2) // SLOTS + 1),
                         2 * i + m // 2)

            def step_features(i, u):
                for h in range(2):
                    sp.wait_ge(st_ready[h], NKT * (SLOTS * i + u + 1))
                features(SLOTS * i + u + SLOTS, u)

            with sp.Fori(0, NB // SLOTS - 1) as i:
                for u in range(SLOTS):
                    step(i, u)
                    step_features(i, u)
            for u in range(SLOTS - 1):
                step(NB // SLOTS - 1, u)

            with sp.Fori(0, NC // 2) as k:
                for p in range(2):
                    sp.wait_ge(o_done, 2 * k + p + 1)
                    sp.dma_start(out_v[:, bass.ds(TC * (2 * k + p), TC), :],
                                 xtc[:, p].rearrange("p k (t d) -> p (k t) d", d=D)).then_inc(o_out[p], 16)
            for p in range(2):
                sp.wait_ge(o_out[p], 16 * NC // 2)

        @block.gpsimd
        def _(pool):
            nc.gpsimd.memset(ident[:], 0.0).then_inc(const_step, 1)
            nc.gpsimd.memset(onesm[:], 1.0 / P).then_inc(const_step, 1)
            for value, tile in ((-0.5, mhalf), (EPS, epst), (0.0, zero)):
                nc.gpsimd.memset(tile[:], value).then_inc(const_step, 1)
            for e in range(E):
                nc.gpsimd.memset(rank[:, e:e + 1], float(E - e)).then_inc(const_step, 1)
            pool.wait_ge(const_step, 5 + E)
            nc.gpsimd.affine_select(out=ident[:], in_=ident[:], compare_op=ALU.not_equal, fill=1.0,
                                    base=0, pattern=[[-1, P]], channel_multiplier=1).then_inc(const_step, 1)

            with pool.Fori(0, NC // 2) as k:
                for p in range(2):
                    c = 2 * k + p
                    pool.wait_ge(mv_done, 2 * (c + 1))
                    nc.gpsimd.tensor_tensor(veps[:], var[:], epst[:, 0:TC], ALU.add).then_inc(veps_done, 1)
                    pool.wait_ge(veps_done, c + 1)
                    nc.gpsimd.tensor_tensor(rstd[:], veps[:], mhalf[:, 0:TC], ALU.pow).then_inc(rstd_done, 1)
                    pool.wait_ge(xn_done, TC * (c + 1))
                    pool.dma_start(xn[:, bass.ds(TC * c, TC), :], xnc[:, p]).then_inc(xn_saved[p], 16)

            with pool.Fori(0, NC) as c:
                for f in range(2):
                    pool.wait_ge(hi_done[f], c + 1)
                    nc.gpsimd.tensor_tensor(dq[f], dq[f],
                                            third[:, f, 0, :], ALU.subtract).then_inc(r1_done[f], 1)
                for f in range(2):
                    pool.wait_ge(mid_done[f], c + 1)
                    nc.gpsimd.tensor_tensor(third[:, f, 2, :], dq[f], third[:, f, 1, :],
                                            ALU.subtract).then_inc(lo_done[f], 1)

            def max_thirds(nth, par, gen):
                for s in range(2):
                    pool.wait_ge(max_done[s], 4 * (nth + 1))
                pool.wait_ge(mt_done, nth - 1 if not isinstance(nth, int) else max(nth - 1, 0))
                c0, c1, c2 = (mpart[:, par, 8 * c:8 * c + 8] for c in range(3))
                nc.gpsimd.tensor_tensor(c0, negm[:, par], zero[:], ALU.add).then_inc(msplit, 1)
                pool.wait_ge(msplit, 4 * nth + 1)
                nc.gpsimd.tensor_tensor(mrest[:, par], negm[:, par], c0, ALU.subtract).then_inc(msplit, 1)
                pool.wait_ge(msplit, 4 * nth + 2)
                nc.gpsimd.tensor_tensor(c1, mrest[:, par], zero[:], ALU.add).then_inc(msplit, 1)
                pool.wait_ge(msplit, 4 * nth + 3)
                nc.gpsimd.tensor_tensor(c2, mrest[:, par], c1, ALU.subtract).then_inc(msplit, 1)

            def residual(pair):
                pool.wait_ge(norm_done, pair + 1)
                nc.gpsimd.tensor_tensor(xn[:, bass.ds(pair, 1), :].rearrange("p o d -> p (o d)"),
                                        xn[:, bass.ds(pair, 1), :].rearrange("p o d -> p (o d)"),
                                        att[:], ALU.add).then_inc(y_done, 1)

            for p in range(2):
                pool.wait_ge(xn_saved[p], 16 * NC // 2)
            max_thirds(0, 0, 0)
            max_thirds(1, 1, 0)

            def pair_of_steps(j, residuals=True, maxima=True):
                if residuals:
                    residual(j - 1)
                if maxima:
                    max_thirds(2 * j + 2, 0, j + 1)
                    max_thirds(2 * j + 3, 1, j + 1)

            pair_of_steps(0, residuals=False)
            with pool.Fori(1, NB // 2 - 1) as j:
                pair_of_steps(j)
            pair_of_steps(NB // 2 - 1, maxima=False)
            residual(NB // 2 - 1)

            pool.wait_ge(fin_d, 6)
            nc.gpsimd.tensor_tensor(brstd[:], bvar[:], mhalf[:, 0:BATCH], ALU.pow).then_inc(fin_pool, 1)

        @block.scalar
        def _(act):
            act.dma_start(wqk[:, 0], wq_t.rearrange("(k p) o -> p k o", p=P)).then_inc(w_small, 16)
            act.dma_start(wqk[:, 1], wk_t.rearrange("(k p) o -> p k o", p=P)).then_inc(w_small, 16)
            act.dma_start(wv[:], wv_t.rearrange("(k p) o -> p k o", p=P)).then_inc(w_small, 16)
            act.dma_start(wg[:], wg_t.rearrange("(k p) e -> p k e", p=P)).then_inc(w_small, 16)

            def xt_out(c, k, p):
                act.wait_ge(lg_ready[p], k)
                act.wait_ge(xt_stored[p], 16 * k)
                for kt in range(KT):
                    act.wait_ge(xt_psum[p], KT * k + kt + 1)
                    nc.scalar.copy(xtc[:, p, kt, :], ps[:, XT_BANK[kt], :]).then_inc(xt_evac, 1)
                act.wait_ge(xt_evac, KT * (c + 1))
                act.dma_start(xt_d[:, :, bass.ds(c * CH, CH)].rearrange("k p t -> p k t"),
                              xtc[:, p]).then_inc(xt_stored[p], 16)

            def qk_out(c):
                act.wait_ge(stage_out, 16 * c)
                for o in range(4):
                    act.wait_ge(qk_ready, 4 * c + o + 1)
                    nc.scalar.copy(stage[:, o, :], ps[:, QK_BANK[o], :]).then_inc(qk_evac, 1)
                act.wait_ge(qk_evac, 4 * (c + 1))
                act.dma_start(qk_d.rearrange("f (k p) t -> p (f k) t", p=P)[:, :, bass.ds(c * CH, CH)],
                              stage[:]).then_inc(stage_out, 16)

            xt_out(0, 0, 0)
            with act.Fori(0, NC // 2 - 1) as k:
                qk_out(2 * k)
                xt_out(2 * k + 1, k, 1)
                qk_out(2 * k + 1)
                xt_out(2 * k + 2, k + 1, 0)
            qk_out(NC - 2)
            xt_out(NC - 1, NC // 2 - 1, 1)
            qk_out(NC - 1)

            act.wait_ge(gap_done, 1)
            nc.scalar.activation(ex[:], gap[:], ACT.Exp).then_inc(gexp_done, 1)

            act.wait_ge(stage_out, 16 * NC)
            with act.Fori(0, NC) as c:
                for f in range(2):
                    act.wait_ge(third_out[f], 48 * c)
                    for b in range(BC):
                        act.dma_start(dq[f][b * DH:(b + 1) * DH].rearrange("d (g t) -> d g t", t=TB),
                                      qk_d[f].rearrange("(g d) t -> d g t", d=DH)
                                      [:, :, bass.ds(c * CH + b * TB, TB)]).then_inc(dq_in[f], 16)
                for f in range(2):
                    act.wait_ge(dq_in[f], 16 * BC * (c + 1))
                    nc.scalar.copy(third[:, f, 0, :], dq[f]).then_inc(hi_done[f], 1)
                for f in range(2):
                    act.wait_ge(r1_done[f], c + 1)
                    nc.scalar.copy(third[:, f, 1, :], dq[f]).then_inc(mid_done[f], 1)
                for f in range(2):
                    act.wait_ge(mid_done[f], c + 1)
                    act.wait_ge(lo_done[f], c + 1)
                    for r in range(3):
                        act.dma_start(third_d[f, r, bass.ds(c * P, P), :], third[:, f, r, :]
                                      ).then_inc(third_out[f], 16)

            act.wait_ge(m_evac, KT * E)

            def exps(n, kt):
                for h in range(2):
                    act.wait_ge(pv_done[kt % 4], 2 * n + kt // 4)
                    act.wait_ge(st_ready[h], NKT * n + kt + 1)
                    nc.scalar.activation(wp[:, kt % 4, h * HALF:(h + 1) * HALF], ps[:, ST_BANK[h], :],
                                         ACT.Exp).then_inc(exp_done[h], 1)

            def pv_out_at(i, u):
                n = SLOTS * i + u
                act.wait_ge(pv_done[3], 2 * n + 2)
                act.wait_ge(tr_done, 2 * i + u // 2)
                nc.scalar.copy(ot[:, :, u % 2, :], ps[:, PV_BANK, 0:4 * TB].rearrange("p (g t) -> p g t", t=TB)
                               ).then_inc(pv_evac, 1)

            def step(i, u, before=True):
                exps(SLOTS * i + u, 0)
                if before:
                    pv_out_at(i if u else i - 1, (u - 1) % SLOTS)
                for kt in range(1, NKT):
                    exps(SLOTS * i + u, kt)

            for u in range(SLOTS):
                step(0, u, before=u > 0)
            with act.Fori(1, NB // SLOTS) as i:
                for u in range(SLOTS):
                    step(i, u)
            pv_out_at(NB // SLOTS - 1, SLOTS - 1)

            act.wait_ge(fin_d, 7)
            with act.Fori(0, BATCH) as b:
                for p in range(2):
                    g = 2 * b + p
                    act.wait_ge(o_done, 2 * b)
                    nc.scalar.activation(xnc[:, p], xn[:, bass.ds(TC * g, TC), :], ACT.Identity,
                                         bias=bshift[:, bass.ds(b, 1)], scale=brstd[:, bass.ds(b, 1)]
                                         ).then_inc(z_done, 1)

        @block.vector
        def _(dve):
            nc.vector.memset(v_all[:, :, :, DH:VW], 1.0).then_inc(ones_done, 1)

            def layernorm(c, k, p):
                dve.wait_ge(x_in[p], 16 * (k + 1))
                for t in range(TC):
                    nc.vector.bn_stats(st[:, t, :], acc[:, bass.ds(TC * c + t, 1), :].rearrange("p o d -> p (o d)")
                                       ).then_inc(stats_done, 1)
                dve.wait_ge(stats_done, TC * (c + 1))
                nc.vector.tensor_tensor(part[:, 0], st[:, :, 1], st[:, :, 4], ALU.add).then_inc(part_done, 1)
                nc.vector.tensor_tensor(part[:, 1], st[:, :, 1], st[:, :, 4], ALU.subtract).then_inc(part_done, 1)
                nc.vector.tensor_tensor(part[:, 2], st[:, :, 2], st[:, :, 5], ALU.add).then_inc(part_done, 1)
                dve.wait_ge(part_done, 4 * c + 3)
                nc.vector.tensor_scalar(mean[:], part[:, 0], 0.5, None, ALU.mult).then_inc(mv_done, 1)
                nc.vector.scalar_tensor_tensor(out=part[:, 3], in0=part[:, 1], scalar=0.25, in1=part[:, 1],
                                               op0=ALU.mult, op1=ALU.mult).then_inc(part_done, 1)
                dve.wait_ge(part_done, 4 * c + 4)
                nc.vector.scalar_tensor_tensor(out=var[:], in0=part[:, 2], scalar=1.0 / D, in1=part[:, 3],
                                               op0=ALU.mult, op1=ALU.add).then_inc(mv_done, 1)
                dve.wait_ge(rstd_done, c + 1)
                dve.wait_ge(xt_psum[p], KT * k)
                dve.wait_ge(xn_saved[p], 16 * k)
                for t in range(TC):
                    nc.vector.tensor_scalar(xnc[:, p, t, :], acc[:, bass.ds(TC * c + t, 1), :].rearrange("p o d -> p (o d)"),
                                            mean[:, t:t + 1], rstd[:, t:t + 1], ALU.subtract, ALU.mult).then_inc(xn_done, 1)
                dve.wait_ge(xn_done, TC * (c + 1))

            def v_and_logits_out(c, k, p):
                for h in range(2):
                    dve.wait_ge(v_ready, 2 * c + h + 1)
                    nc.vector.tensor_copy(v_all[:, bass.ds(BC * c + 4 * h, 4), :, 0:DH],
                                          ps[:, V_BANK[h], :].rearrange("p (b k d) -> p b k d", b=4, k=NKT)
                                          ).then_inc(v_evac, 1)
                dve.wait_ge(lg_ready[p], k + 1)
                nc.vector.tensor_copy(lg[:, bass.ds(TC * c, TC), :],
                                      ps[:, G_BANK, 0:TC * E].rearrange("p (t e) -> p t e", e=E)).then_inc(lg_evac, 1)

            layernorm(0, 0, 0)
            with dve.Fori(0, NC // 2 - 1) as k:
                layernorm(2 * k + 1, k, 1)
                v_and_logits_out(2 * k, k, 0)
                layernorm(2 * k + 2, k + 1, 0)
                v_and_logits_out(2 * k + 1, k, 1)
            layernorm(NC - 1, NC // 2 - 1, 1)
            v_and_logits_out(NC - 2, NC // 2 - 1, 0)
            v_and_logits_out(NC - 1, NC // 2 - 1, 1)

            steps = [0]

            def g(instruction):
                instruction.then_inc(gate_step, 1)
                steps[0] += 1
                dve.wait_ge(gate_step, steps[0])

            def wide(a):
                return a[:].unsqueeze(2).to_broadcast([P, NT, E])

            dve.wait_ge(lg_evac, NC)
            dve.wait_ge(const_step, 6 + E)

            def pick(logits, top, onehot):
                g(nc.vector.reduce_max(top[:], logits[:], AX.X))
                g(nc.vector.tensor_tensor(eq[:], logits[:], wide(top), ALU.is_equal))
                g(nc.vector.tensor_tensor(eq[:], eq[:], rank[:].unsqueeze(1).to_broadcast([P, NT, E]), ALU.mult))
                g(nc.vector.reduce_max(first[:], eq[:], AX.X))
                g(nc.vector.tensor_tensor(onehot[:], eq[:], wide(first), ALU.is_equal))

            pick(lg, top1, oh1)
            g(nc.vector.scalar_tensor_tensor(out=lm[:], in0=oh1[:], scalar=-BIG, in1=lg[:], op0=ALU.mult, op1=ALU.add))
            pick(lm, top2, oh2)
            nc.vector.tensor_tensor(gap[:], top2[:], top1[:], ALU.subtract).then_inc(gap_done, 1)
            dve.wait_ge(gexp_done, 1)
            g(nc.vector.tensor_scalar(gs[:], ex[:], 1.0, None, ALU.add))
            g(nc.vector.reciprocal(g1[:], gs[:]))
            g(nc.vector.tensor_tensor(g2[:], ex[:], g1[:], ALU.mult))
            g(nc.vector.tensor_tensor(lm[:], oh1[:], wide(g1), ALU.mult))
            g(nc.vector.tensor_tensor(eq[:], oh2[:], wide(g2), ALU.mult))
            nc.vector.tensor_tensor(gates[:], lm[:], eq[:], ALU.add).then_inc(gates_done, 1)

            with dve.Fori(0, E // 2) as k:
                for q in range(2):
                    for dh in range(KT):
                        dve.wait_ge(m_ready[q], KT * k + dh + 1)
                        nc.vector.tensor_copy(mt[:, dh, bass.ds(2 * k + q, 1), :].rearrange("p o d -> p (o d)"),
                                              ps[:, 2 * q + dh, 0:D]).then_inc(m_evac, 1)

            dve.wait_ge(gates_done, 1)
            with dve.Fori(0, NT // 2) as k:
                for p in range(2):
                    tile = acc[:, bass.ds(2 * k + p, 1), :].rearrange("p o d -> p (o d)")
                    for e in range(E):
                        if e % 2 == 0:
                            dve.wait_ge(y_ready[p], 4 * k + e // 2 + 1)
                        dve.wait_ge(ff_step[p], E * k + e)
                        nc.vector.scalar_tensor_tensor(
                            out=tile, in0=ps[:, 4 * p + e // 2, (e % 2) * D:(e % 2 + 1) * D],
                            scalar=gates[:, bass.ds(2 * k + p, 1), e:e + 1].rearrange("p o e -> p (o e)"),
                            in1=tile, op0=ALU.mult, op1=ALU.add).then_inc(ff_step[p], 1)

            for p in range(2):
                dve.wait_ge(ff_step[p], E * NT // 2)
            nc.vector.memset(kf[FR:SR, :, :], 1.0).then_inc(att_const, 1)
            nc.vector.memset(ps[:, PV_BANK, :], 0.0).then_inc(att_const, 1)
            nc.vector.memset(mpart[:], 0.0).then_inc(att_const, 1)

            def maxima(nth, slot_gen, par, qt):
                if qt == 0 and slot_gen is not None:
                    dve.wait_ge(msplit, slot_gen)
                dve.wait_ge(max_ready[qt % 2], 4 * nth + qt // 2 + 1)
                b = MAX_BANK[qt % 2]
                nc.vector.tensor_reduce(negm[:, par, qt:qt + 1], ps[:, b:b + 2, :].rearrange("p b c -> p (b c)"),
                                        AX.X, ALU.max, negate=True).then_inc(max_done[qt % 2], 1)

            def max_transpose(nth, par, gen):
                dve.wait_ge(msplit, 4 * (nth + 1))
                dve.wait_ge(mrow_out[par], 16 * gen)
                nc.vector.transpose(mt32[:, par], mpart[:, par]).then_inc(mt_done, 1)

            def normalise(pair):
                dve.wait_ge(tr_done, pair + 1)
                o = ps[:, TR_BANK, :].rearrange("p (g c v) -> p g c v", g=4, c=4)
                nc.vector.reciprocal(rden[:], o[:, :, :, DH]).then_inc(rden_done, 1)
                dve.wait_ge(rden_done, pair + 1)
                dve.wait_ge(y_done, pair)
                nc.vector.tensor_tensor(att[:].rearrange("p (c g d) -> p g c d", c=4, g=4), o[:, :, :, 0:DH],
                                        rden[:].unsqueeze(3).to_broadcast([P, 4, 4, DH]), ALU.mult
                                        ).then_inc(norm_done, 1)

            def statistics(pair):
                dve.wait_ge(y_done, pair + 1)
                nc.vector.bn_stats(ystat[:, bass.ds(pair, 1), :].rearrange("p o s -> p (o s)"),
                                   xn[:, bass.ds(pair, 1), :].rearrange("p o d -> p (o d)")).then_inc(ystat_done, 1)

            def step(i, u, pair=None, has_max=True, has_rows=True):
                n = SLOTS * i + u
                for qt in range(NKT):
                    if has_max:
                        maxima(n + 2, 4 * (n + 1), u % 2, qt)
                    if qt == 1 and has_rows:
                        max_transpose(n + 1, (u + 1) % 2, 2 * i + (u + 1) // 2)
                    if qt == 4 and pair is not None:
                        normalise(pair)
                    if qt == 6 and pair is not None:
                        statistics(pair)

            dve.wait_ge(att_const, 3)
            for n in range(2):
                for qt in range(NKT):
                    maxima(n, None, n, qt)
                if n == 0:
                    max_transpose(0, 0, 0)
            for u in range(SLOTS):
                step(0, u, pair=0 if u == 2 else None)
            with dve.Fori(1, NB // SLOTS - 1) as i:
                for u in range(SLOTS):
                    step(i, u, pair=2 * i + u // 2 - 1 if u % 2 == 0 else None)
            last = NB // SLOTS - 1
            for u in range(SLOTS):
                step(last, u, pair=2 * last + u // 2 - 1 if u % 2 == 0 else None,
                     has_max=u < 2, has_rows=u < 3)
            normalise(NB // 2 - 1)
            statistics(NB // 2 - 1)

            dve.wait_ge(ystat_done, NT)
            for b in range(BATCH):
                last_aggr = nc.vector.bn_aggr(bmv[:, b, :], ystat[:, b * TPB:(b + 1) * TPB, :].rearrange("p t s -> p (t s)"))
            last_aggr.then_inc(fin_d, 1)
            dve.wait_ge(fin_pe, 1)
            nc.vector.tensor_copy(bmean[:], ps[:, 0, 0:2 * BATCH].rearrange("p (b s) -> p b s", s=2)).then_inc(fin_d, 1)
            dve.wait_ge(fin_d, 2)
            nc.vector.tensor_tensor(dev2[:], bmv[:, :, 0], bmean[:, :, 0], ALU.subtract).then_inc(fin_d, 1)
            dve.wait_ge(fin_d, 3)
            nc.vector.tensor_tensor(dev2[:], dev2[:], dev2[:], ALU.mult).then_inc(fin_d, 1)
            dve.wait_ge(fin_pe, 2)
            nc.vector.tensor_tensor(bvar[:], bmean[:, :, 1], ps[:, 1, 0:BATCH], ALU.add).then_inc(fin_d, 1)
            dve.wait_ge(fin_d, 5)
            nc.vector.tensor_scalar(bvar[:], bvar[:], EPS, None, ALU.add).then_inc(fin_d, 1)
            dve.wait_ge(fin_pool, 1)
            nc.vector.scalar_tensor_tensor(out=bshift[:], in0=bmean[:, :, 0], scalar=-1.0, in1=brstd[:],
                                           op0=ALU.mult, op1=ALU.mult).then_inc(fin_d, 1)
            with dve.Fori(0, NC // 2) as k:
                for p in range(2):
                    dve.wait_ge(z_done, 2 * k + p + 1)
                    dve.wait_ge(o_out[p], 16 * k)
                    nc.vector.tensor_tensor(xtc[:, p].rearrange("p k (t d) -> p (k t) d", d=D), xnc[:, p],
                                            acc[:, bass.ds(TC * (2 * k + p), TC), :], ALU.add).then_inc(o_done, 1)

        @block.tensor
        def _(pe):
            def transposes(c, k, p):
                pe.wait_ge(xn_done, TC * (c + 1))
                pe.wait_ge(xt_evac, KT * c)
                for kt in range(KT):
                    for t in range(TC):
                        last = nc.tensor.transpose(ps[:, XT_BANK[kt], t * P:(t + 1) * P],
                                                   xnc[:, p, t, kt * P:(kt + 1) * P], ident[:])
                    last.then_inc(xt_psum[p], 1)

            def project_qk(c, p):
                pe.wait_ge(xt_evac, KT * (c + 1))
                for o in range(4):
                    pe.wait_ge(qk_evac, 4 * c + o // 3)
                    for kt in range(KT):
                        last = nc.tensor.matmul(ps[:, QK_BANK[o], :], wqk[:, o // 2, kt, (o % 2) * P:(o % 2 + 1) * P],
                                                xtc[:, p, kt, :], start=kt == 0, stop=kt == KT - 1)
                    last.then_inc(qk_ready, 1)

            def project_v(c, p):
                pe.wait_ge(v_evac, 2 * c)
                for h in range(2):
                    for b in range(4):
                        for par in range(2):
                            for kt in range(KT):
                                w = wv[:, kt, :].rearrange("p (g o d) -> p o g d", o=2, d=DH)[:, par]
                                last = nc.tensor.matmul(
                                    ps[par * TB:(par + 1) * TB, V_BANK[h], b * P:(b + 1) * P],
                                    xtc[:, p, kt, (4 * h + b) * TB:(4 * h + b + 1) * TB], w,
                                    start=kt == 0, stop=kt == KT - 1, tile_position=(0, par * TB))
                    last.then_inc(v_ready, 1)

            def logits(c, p):
                pe.wait_ge(lg_evac, c)
                for t in range(TC):
                    for kt in range(KT):
                        last = nc.tensor.matmul(ps[:, G_BANK, t * E:(t + 1) * E], xtc[:, p, kt, t * P:(t + 1) * P],
                                                wg[:, kt, :], start=kt == 0, stop=kt == KT - 1)
                last.then_inc(lg_ready[p], 1)

            pe.wait_ge(const_step, 6 + E)
            transposes(0, 0, 0)
            pe.wait_ge(w_small, 64)
            with pe.Fori(0, NC // 2 - 1) as k:
                for p in range(2):
                    project_qk(2 * k + p, p)
                    transposes(2 * k + p + 1, k + p, 1 - p)
                    project_v(2 * k + p, p)
                    logits(2 * k + p, p)
            for p in range(2):
                c = NC - 2 + p
                project_qk(c, p)
                if p == 0:
                    transposes(c + 1, NC // 2 - 1, 1)
                project_v(c, p)
                logits(c, p)

            pe.wait_ge(xt_evac, KT * NC)
            pe.wait_ge(qk_evac, 4 * NC)
            with pe.Fori(0, E // 2) as k:
                for q in range(2):
                    pe.wait_ge(m_evac, 2 * KT * k)
                    for s in range(2):
                        pe.wait_ge(w_in_s[s], 32 * (2 * k + q + 1))
                        for dh in range(KT):
                            for h in range(HU):
                                last = nc.tensor.matmul(ps[:, 2 * q + dh, 0:D], win[s][:, h, dh * P:(dh + 1) * P],
                                                        wout[s][:, h, :], start=s == 0 and h == 0,
                                                        stop=s == 1 and h == HU - 1)
                            if s == 1:
                                last.then_inc(m_ready[q], 1)
                            elif dh == KT - 1:
                                last.then_inc(first_half, 1)

            pe.wait_ge(m_evac, KT * E)
            pe.wait_ge(v_evac, 2 * NC)
            pe.wait_ge(lg_evac, NC)
            with pe.Fori(0, NT // 2) as k:
                for p in range(2):
                    pe.wait_ge(xtt_in[p], 16 * (k + 1))
                    pe.wait_ge(ff_step[p], E * k)
                    for j in range(E // 2):
                        for kt in range(KT):
                            last = nc.tensor.matmul(ps[:, 4 * p + j, :], xtt[:, p, kt, :],
                                                    mt[:, kt, 2 * j:2 * j + 2, :].rearrange("p e d -> p (e d)"),
                                                    start=kt == 0, stop=kt == KT - 1)
                        last.then_inc(y_ready[p], 1)

            def max_scores(i, u, n, qt):
                if qt == 0:
                    pe.wait_ge(feat_in[u], 192 * (i + 1))
                pe.wait_ge(max_done[qt % 2], 4 * n + qt // 2)
                for h in range(2):
                    last = nc.tensor.matmul(ps[:, MAX_BANK[qt % 2] + h, :], qf[0:FR, u, qt * P:(qt + 1) * P],
                                            kf[0:FR, u, h * HALF:(h + 1) * HALF], start=True, stop=True)
                last.then_inc(max_ready[qt % 2], 1)

            def scores(i, u, n, kt):
                if kt == 0:
                    pe.wait_ge(mrow_in[u], 48 * (i + 1))
                for h in range(2):
                    pe.wait_ge(exp_done[h], NKT * n + kt)
                    nc.tensor.matmul(ps[:, ST_BANK[h], :], kf[0:SR, u, kt * P:(kt + 1) * P],
                                     qf[0:SR, u, h * HALF:(h + 1) * HALF], start=True, stop=True
                                     ).then_inc(st_ready[h], 1)

            def sum_values(n, par, gen, kt):
                if kt == 0:
                    pe.wait_ge(vb_in[par], 16 * (gen + 1))
                    pe.wait_ge(pv_evac, n)
                for h in range(2):
                    pe.wait_ge(exp_done[h], NKT * n + kt + 1)
                for j in range(4):
                    last = nc.tensor.matmul(ps[32 * j:32 * j + VW, PV_BANK, 0:POS // 4], vb[:, par, kt, :],
                                            wp[:, kt % 4, j * (POS // 4):(j + 1) * (POS // 4)],
                                            start=kt == 0, stop=kt == NKT - 1, tile_position=(0, 32 * j))
                last.then_inc(pv_done[kt % 4], 1)

            def to_token_rows(pair):
                pe.wait_ge(pv_evac, 2 * pair + 2)
                pe.wait_ge(norm_done, pair)
                for g in range(4):
                    last = nc.tensor.transpose(ps[:, TR_BANK, g * P:(g + 1) * P],
                                               ot[:, g].rearrange("p b t -> p (b t)"), ident[:])
                last.then_inc(tr_done, 1)

            def step(i, u, pair=None, before=True, has_max=True):
                n = SLOTS * i + u
                for kt in range(NKT):
                    scores(i, u, n, kt)
                    if has_max:
                        max_scores(i + (u + 2) // SLOTS, (u + 2) % SLOTS, n + 2, kt)
                    if kt:
                        sum_values(n, u % 2, 2 * i + u // 2, kt - 1)
                    elif before:
                        sum_values(n - 1, (u - 1) % 2, 2 * i + (u - 1) // 2, NKT - 1)
                    if kt == 2 and pair is not None:
                        to_token_rows(pair)

            for p in range(2):
                pe.wait_ge(ff_step[p], E * NT // 2)
            pe.wait_ge(att_const, 3)
            for n in range(2):
                for qt in range(NKT):
                    max_scores(0, n, n, qt)
            for u in range(SLOTS):
                step(0, u, pair=0 if u == 2 else None, before=u > 0)
            with pe.Fori(1, NB // SLOTS - 1) as i:
                for u in range(SLOTS):
                    step(i, u, pair=2 * i + u // 2 - 1 if u % 2 == 0 else None)
            last_i = NB // SLOTS - 1
            for u in range(SLOTS):
                step(last_i, u, pair=2 * last_i + u // 2 - 1 if u % 2 == 0 else None, has_max=u < 2)
            sum_values(NB - 1, 1, NB // 2 - 1, NKT - 1)
            to_token_rows(NB // 2 - 1)

            pe.wait_ge(fin_d, 1)
            nc.tensor.matmul(ps[:, 0, 0:2 * BATCH], onesm[:], bmv[:].rearrange("p b s -> p (b s)"),
                             start=True, stop=True).then_inc(fin_pe, 1)
            pe.wait_ge(fin_d, 4)
            nc.tensor.matmul(ps[:, 1, 0:BATCH], onesm[:], dev2[:], start=True, stop=True).then_inc(fin_pe, 1)


def build(nc, arrays, out_shape):
    args = [nc.dram_tensor(name, a.shape, mybir.dt.from_np(a.dtype), kind="ExternalInput").ap()
            for name, a in arrays.items()]
    result = nc.dram_tensor("result", out_shape, FP32, kind="ExternalOutput").ap()
    attention_and_experts(nc, *args, result)


def kernel(L0_attn_x, L0_attn_Wq, L0_attn_Wk, L0_attn_Wv, L0_ffn_w_gate, L0_ffn_w_in, L0_ffn_w_out):
    import numpy as np
    import concourse.bacc as bacc
    from concourse.bass_utils import run_bass_kernel_spmd

    def laid_out(a, axes=None):
        a = np.asarray(a)
        return np.ascontiguousarray(a if axes is None else np.transpose(a, axes))

    arrays = {
        "x": laid_out(L0_attn_x),
        "wq_t": laid_out(L0_attn_Wq, (1, 0)),
        "wk_t": laid_out(L0_attn_Wk, (1, 0)),
        "wv_t": laid_out(L0_attn_Wv, (1, 0)),
        "wg_t": laid_out(L0_ffn_w_gate, (1, 0)),
        "w_in": laid_out(L0_ffn_w_in),
        "w_out_t": laid_out(L0_ffn_w_out, (0, 2, 1)),
    }
    nc = bacc.Bacc("TRN2", target_bir_lowering=False, num_devices=1)
    build(nc, arrays, arrays["x"].shape)
    r = run_bass_kernel_spmd(nc, [arrays], core_ids=[0])
    return r.results[0]["result"]
```

```python
import concourse.bass as bass
from concourse import mybir
from contextlib import ExitStack


FP32 = mybir.dt.float32
FP32R = mybir.dt.float32r
BF16 = mybir.dt.bfloat16
ALU = mybir.AluOpType
ACT = mybir.ActivationFunctionType
AX = mybir.AxisListType

P = 128
EPS = 1e-5
BIG = 3e38


def attention_and_experts(nc, x, wq_t, wk_t, wv_t, wg_t, w_in, w_out_t, out):
    BATCH, S, D = x.shape
    T = BATCH * S
    NT = T // P
    KT = D // P
    HEADS = 16
    DH = D // HEADS
    NB = HEADS * BATCH
    TB = T // NB
    G = D // DH
    POS = TB * G
    NKT = POS // P
    HALF = POS // 2
    TC = 4
    CH = TC * P
    NC = T // CH
    BC = CH // TB
    E, HID, _ = w_in.shape
    HU = HID // 2 // P
    VW = DH + 1
    TERMS_Q = (0, 1, 2, 0, 1, 0)
    TERMS_K = (0, 0, 0, 1, 1, 2)
    FR = DH * len(TERMS_Q)
    SR = FR + 3
    SLOTS = 4
    TPB = NT // BATCH

    x_v = x.rearrange("a (t p) d -> p (a t) d", p=P)
    out_v = out.rearrange("a (t p) d -> p (a t) d", p=P)

    qk_d = nc.dram_tensor("qk_d", [2, KT * P, T], FP32, kind="Internal").ap()
    third_d = nc.dram_tensor("third_d", [2, 3, NB * DH, POS], BF16, kind="Internal").ap()
    xth_d = nc.dram_tensor("xth_d", [KT, P, T], FP32, kind="Internal").ap()
    xtl_d = nc.dram_tensor("xtl_d", [KT, P, T], FP32, kind="Internal").ap()
    v_d = nc.dram_tensor("v_d", [P, NB, NKT, VW], FP32, kind="Internal").ap()
    max_d = nc.dram_tensor("max_d", [2, P, 32], BF16, kind="Internal").ap()

    ctx = ExitStack()
    with ctx:
        def sb(name, shape, dt=FP32):
            return ctx.enter_context(nc.sbuf_tensor(name, shape, dt))

        def sem(name, n=None):
            if n is None:
                return ctx.enter_context(nc.semaphore(name))
            return [ctx.enter_context(nc.semaphore(f"{name}{i}")) for i in range(n)]

        acc = sb("acc", [P, NT, D])
        xn = sb("xn", [P, NT, D])
        mth = sb("mth", [P, KT, E, D], FP32R)
        mtl = sb("mtl", [P, KT, E, D], FP32R)
        wqk = sb("wqk", [P, 2, KT, D])
        wqkh = sb("wqkh", [P, 2, KT, D], FP32R)
        wqkl = sb("wqkl", [P, 2, KT, D], FP32R)
        wv = sb("wv", [P, KT, D])
        wg = sb("wg", [P, KT, E])
        ident = sb("ident", [P, P])
        onesm = sb("onesm", [P, P])
        xnc = sb("xnc", [P, 2, TC, D])
        xtc = sb("xtc", [P, 2, KT, CH])
        xth = sb("xth", [P, 2, KT, CH], FP32R)
        xtl = sb("xtl", [P, 2, KT, CH], FP32R)
        stage = sb("stage", [P, 2 * KT, CH])
        vstage = sb("vstage", [P, BC, NKT, VW])
        st = sb("st", [P, TC, 6])
        part = sb("part", [P, 4, TC])
        mean = sb("mean", [P, TC])
        var = sb("var", [P, TC])
        veps = sb("veps", [P, TC])
        rstd = sb("rstd", [P, TC])
        mhalf = sb("mhalf", [P, 8])
        epst = sb("epst", [P, 8])
        zero = sb("zero", [P, 8])
        lg = sb("lg", [P, NT, E])
        rank = sb("rank", [P, E])
        eq = sb("eq", [P, NT, E])
        oh1 = sb("oh1", [P, NT, E])
        oh2 = sb("oh2", [P, NT, E])
        lm = sb("lm", [P, NT, E])
        gates = sb("gates", [P, NT, E])
        top1 = sb("top1", [P, NT])
        top2 = sb("top2", [P, NT])
        first = sb("first", [P, NT])
        gap = sb("gap", [P, NT])
        ex = sb("ex", [P, NT])
        gs = sb("gs", [P, NT])
        g1 = sb("g1", [P, NT])
        g2 = sb("g2", [P, NT])
        xtth = sb("xtth", [P, 2, KT, P], FP32R)
        xttl = sb("xttl", [P, 2, KT, P], FP32R)
        wp = sb("wp", [P, 4, POS])
        win = [wp[:, 2 * s, :].rearrange("p (h d) -> p h d", h=HU) for s in range(2)]
        wout = [wp[:, 2 * s + 1, :].rearrange("p (h d) -> p h d", h=HU) for s in range(2)]
        dq = [[stage[:, 2 * f:2 * f + 2, :].rearrange("p k t -> p (k t)") for f in range(2)],
              [xnc[:, f].rearrange("p t d -> p (t d)") for f in range(2)]]
        room = [wp[:, i, :] for i in range(4)] + [xtc[:, i].rearrange("p k t -> p (k t)") for i in range(2)]
        room = [r.bitcast(BF16)[:, h * POS:(h + 1) * POS] for r in room for h in range(2)]
        third = [[room[6 * p + 3 * f:6 * p + 3 * f + 3] for f in range(2)] for p in range(2)]
        qf = sb("qf", [SR, SLOTS, POS], BF16)
        kf = sb("kf", [SR, SLOTS, POS], BF16)
        vb = sb("vb", [P, 2, NKT, VW])
        negm = sb("negm", [P, 2, NKT])
        mrest = sb("mrest", [P, 2, NKT])
        mpart = sb("mpart", [P, 2, 32], BF16)
        mt32 = sb("mt32", [P, 2, 32], BF16)
        ot = sb("ot", [P, 4, 2, TB])
        rden = sb("rden", [P, 4, 4])
        att = sb("att", [P, D])
        ystat = sb("ystat", [P, NT, 6])
        bmv = sb("bmv", [P, BATCH, 2])
        dev2 = sb("dev2", [P, BATCH])
        bmean = sb("bmean", [P, BATCH, 2])
        bvar = sb("bvar", [P, BATCH])
        brstd = sb("brstd", [P, BATCH])
        bshift = sb("bshift", [P, BATCH])

        ps = ctx.enter_context(nc.psum_tensor("ps", [P, 8, 512], FP32))
        XT_BANK = (0, 1)
        QK_BANK = (2, 3, 2, 3)
        V_BANK = (5, 6)
        G_BANK = 7
        M_BANK = (4, 7)
        MAX_BANK = (0, 2)
        ST_BANK = (4, 5)
        PV_BANK = 6
        TR_BANK = 7

        w_small = sem("w_small")
        x_in = sem("x_in", 2)
        const_step = sem("const_step")
        stats_done = sem("stats_done")
        part_done = sem("part_done")
        mv_done = sem("mv_done")
        veps_done = sem("veps_done")
        rstd_done = sem("rstd_done")
        xn_done = sem("xn_done")
        xn_saved = sem("xn_saved", 2)
        xt_psum = sem("xt_psum", 2)
        xt_evac = sem("xt_evac")
        xth_done = sem("xth_done")
        xtl_done = sem("xtl_done")
        wqk_split = sem("wqk_split")
        xt_stored = sem("xt_stored", 2)
        qk_ready = sem("qk_ready")
        qk_evac = sem("qk_evac")
        stage_out = sem("stage_out")
        v_ready = sem("v_ready", 2)
        v_evac = sem("v_evac")
        ones_done = sem("ones_done")
        v_stored = sem("v_stored")
        lg_ready = sem("lg_ready")
        lg_evac = sem("lg_evac")
        gate_step = sem("gate_step")
        gap_done = sem("gap_done")
        gexp_done = sem("gexp_done")
        gates_done = sem("gates_done")
        dq_in = sem("dq_in", 4)
        hi_done = sem("hi_done", 2)
        r1_done = sem("r1_done", 2)
        mid_done = sem("mid_done", 2)
        lo_done = sem("lo_done", 2)
        third_out = sem("third_out", 4)
        w_in_s = sem("w_in_s", 2)
        first_half = sem("first_half")
        m_ready = sem("m_ready")
        mh_done = sem("mh_done")
        ml_done = sem("ml_done")
        xtt_in = sem("xtt_in", 2)
        y_ready = sem("y_ready", 2)
        ff_step = sem("ff_step", 2)
        att_const = sem("att_const")
        feat_in = sem("feat_in", SLOTS)
        vb_in = sem("vb_in", 2)
        st_ready = sem("st_ready", 2)
        exp_done = sem("exp_done", 2)
        pv_done = sem("pv_done", 4)
        pv_evac = sem("pv_evac")
        max_ready = sem("max_ready", 2)
        max_done = sem("max_done", 2)
        msplit = sem("msplit")
        mt_done = sem("mt_done")
        mrow_out = sem("mrow_out", 2)
        mrow_in = sem("mrow_in", SLOTS)
        tr_done = sem("tr_done")
        rden_done = sem("rden_done")
        norm_done = sem("norm_done")
        y_done = sem("y_done")
        ystat_done = sem("ystat_done")
        fin_d = sem("fin_d")
        fin_pe = sem("fin_pe")
        fin_pool = sem("fin_pool")
        z_done = sem("z_done")
        o_done = sem("o_done")
        o_out = sem("o_out", 2)

        def feature_loads(n):
            block_rows = bass.ds(n * DH, DH)
            for first_row, terms in ((0, 3), (3, 2), (5, 1)):
                rows = slice(first_row * DH, (first_row + terms) * DH)
                yield qf, rows, third_d[0, 0:terms, block_rows, :]
                yield kf, rows, third_d[1, first_row // 2 if terms < 3 else 0, block_rows, :
                                        ].unsqueeze(0).to_broadcast([terms, DH, POS])

        block = ctx.enter_context(nc.Block())

        @block.sync
        def _(sp):
            def load_x(c, k, p):
                sp.wait_ge(x_in[p], 16 * k)
                sp.dma_start(acc[:, bass.ds(TC * c, TC), :], x_v[:, bass.ds(TC * c, TC), :]).then_inc(x_in[p], 16)

            def load_weights(e):
                for s in range(2):
                    if s == 0:
                        sp.wait_ge(first_half, e)
                    else:
                        sp.wait_ge(ml_done, KT * e)
                    rows = bass.ds(e * HID + s * HU * P, HU * P)
                    sp.dma_start(win[s], w_in.rearrange("e h d -> (e h) d")[rows, :]
                                 .rearrange("(p h) d -> p h d", h=HU)).then_inc(w_in_s[s], 16)
                    sp.dma_start(wout[s], w_out_t.rearrange("e h d -> (e h) d")[rows, :]
                                 .rearrange("(p h) d -> p h d", h=HU)).then_inc(w_in_s[s], 16)

            load_x(0, 0, 0)
            load_weights(0)
            load_x(1, 0, 1)
            with sp.Fori(1, NC // 2) as k:
                load_weights(2 * k - 1)
                load_x(2 * k, k, 0)
                load_weights(2 * k)
                load_x(2 * k + 1, k, 1)
            load_weights(E - 1)
            for p in range(2):
                sp.wait_ge(xt_stored[p], 32 * NC // 2)
            with sp.Fori(0, NT // 2) as k:
                for p in range(2):
                    sp.wait_ge(y_ready[p], 4 * k)
                    for half, src in ((xtth, xth_d), (xttl, xtl_d)):
                        sp.dma_start(half[:, p].bitcast(FP32), src[:, :, bass.ds((2 * k + p) * P, P)]
                                     .rearrange("k p t -> p k t")).then_inc(xtt_in[p], 16)

            def features(n, slot):
                for dst, rows, source in feature_loads(n):
                    sp.dma_start(dst[rows, slot, :], source).then_inc(feat_in[slot], 16)

            def values(n, par):
                sp.dma_start(vb[:, par], v_d[:, bass.ds(n, 1)].rearrange("p b k v -> p (b k) v")
                             ).then_inc(vb_in[par], 16)

            def max_rows(slot, par, nth, gen_in, gen_slot):
                sp.wait_ge(mt_done, nth + 1)
                sp.wait_ge(mrow_in[(slot + 2) % SLOTS], 16 * gen_in)
                sp.dma_start(max_d[par], mt32[:, par]).then_inc(mrow_out[par], 16)
                sp.wait_ge(mrow_out[par], 16 * (gen_slot + 1))
                for c in range(3):
                    sp.dma_start(qf[FR + c:FR + c + 1, slot, :].rearrange("o (t q r) -> o t q r", q=4, r=32),
                                 max_d[par].rearrange("(q c t) r -> c t q r", q=4, c=4)[c:c + 1]
                                 ).then_inc(mrow_in[slot], 16)

            max_rows(0, 0, 0, 0, 0)

            def step(i, u):
                n = SLOTS * i + u
                sp.wait_ge(pv_done[3], 2 * n)
                values(n + 1, (u + 1) % 2)
                m = u + 1
                max_rows(m % SLOTS, m % 2, n + 1, 3 * (i if u == 0 else i + (m - 2) // SLOTS + 1),
                         2 * i + m // 2)

            def step_features(i, u):
                for h in range(2):
                    sp.wait_ge(st_ready[h], NKT * (SLOTS * i + u + 1))
                features(SLOTS * i + u + SLOTS, u)

            with sp.Fori(0, NB // SLOTS - 1) as i:
                for u in range(SLOTS):
                    step(i, u)
                    step_features(i, u)
            for u in range(SLOTS - 1):
                step(NB // SLOTS - 1, u)

            with sp.Fori(0, NC // 2) as k:
                for p in range(2):
                    sp.wait_ge(o_done, 2 * k + p + 1)
                    sp.dma_start(out_v[:, bass.ds(TC * (2 * k + p), TC), :],
                                 xtc[:, p].rearrange("p k (t d) -> p (k t) d", d=D)).then_inc(o_out[p], 16)
            for p in range(2):
                sp.wait_ge(o_out[p], 16 * NC // 2)

        @block.gpsimd
        def _(pool):
            nc.gpsimd.memset(ident[:], 0.0).then_inc(const_step, 1)
            nc.gpsimd.memset(onesm[:], 1.0 / P).then_inc(const_step, 1)
            for value, tile in ((-0.5, mhalf), (EPS, epst), (0.0, zero)):
                nc.gpsimd.memset(tile[:], value).then_inc(const_step, 1)
            for e in range(E):
                nc.gpsimd.memset(rank[:, e:e + 1], float(E - e)).then_inc(const_step, 1)
            pool.wait_ge(const_step, 5 + E)
            nc.gpsimd.affine_select(out=ident[:], in_=ident[:], compare_op=ALU.not_equal, fill=1.0,
                                    base=0, pattern=[[-1, P]], channel_multiplier=1).then_inc(const_step, 1)

            with pool.Fori(0, NC // 2) as k:
                for p in range(2):
                    c = 2 * k + p
                    pool.wait_ge(mv_done, 2 * (c + 1))
                    nc.gpsimd.tensor_tensor(veps[:], var[:], epst[:, 0:TC], ALU.add).then_inc(veps_done, 1)
                    pool.wait_ge(veps_done, c + 1)
                    nc.gpsimd.tensor_tensor(rstd[:], veps[:], mhalf[:, 0:TC], ALU.pow).then_inc(rstd_done, 1)
                    pool.wait_ge(xn_done, TC * (c + 1))
                    pool.dma_start(xn[:, bass.ds(TC * c, TC), :], xnc[:, p]).then_inc(xn_saved[p], 16)

            with pool.Fori(0, NC // 2) as k:
                for p in range(2):
                    for f in range(2):
                        pool.wait_ge(hi_done[f], 2 * k + p + 1)
                        nc.gpsimd.tensor_tensor(dq[p][f], dq[p][f], third[p][f][0], ALU.subtract).then_inc(r1_done[f], 1)
                    for f in range(2):
                        pool.wait_ge(mid_done[f], 2 * k + p + 1)
                        nc.gpsimd.tensor_tensor(third[p][f][2], dq[p][f], third[p][f][1],
                                                ALU.subtract).then_inc(lo_done[f], 1)

            def max_thirds(nth, par, gen):
                for s in range(2):
                    pool.wait_ge(max_done[s], 4 * (nth + 1))
                pool.wait_ge(mt_done, nth - 1 if not isinstance(nth, int) else max(nth - 1, 0))
                c0, c1, c2 = (mpart[:, par, 8 * c:8 * c + 8] for c in range(3))
                nc.gpsimd.tensor_tensor(c0, negm[:, par], zero[:], ALU.add).then_inc(msplit, 1)
                pool.wait_ge(msplit, 4 * nth + 1)
                nc.gpsimd.tensor_tensor(mrest[:, par], negm[:, par], c0, ALU.subtract).then_inc(msplit, 1)
                pool.wait_ge(msplit, 4 * nth + 2)
                nc.gpsimd.tensor_tensor(c1, mrest[:, par], zero[:], ALU.add).then_inc(msplit, 1)
                pool.wait_ge(msplit, 4 * nth + 3)
                nc.gpsimd.tensor_tensor(c2, mrest[:, par], c1, ALU.subtract).then_inc(msplit, 1)

            def residual(pair):
                pool.wait_ge(norm_done, pair + 1)
                nc.gpsimd.tensor_tensor(xn[:, bass.ds(pair, 1), :].rearrange("p o d -> p (o d)"),
                                        xn[:, bass.ds(pair, 1), :].rearrange("p o d -> p (o d)"),
                                        att[:], ALU.add).then_inc(y_done, 1)

            for p in range(2):
                pool.wait_ge(xn_saved[p], 16 * NC // 2)
            max_thirds(0, 0, 0)
            max_thirds(1, 1, 0)

            def pair_of_steps(j, residuals=True, maxima=True):
                if residuals:
                    residual(j - 1)
                if maxima:
                    max_thirds(2 * j + 2, 0, j + 1)
                    max_thirds(2 * j + 3, 1, j + 1)

            pair_of_steps(0, residuals=False)
            with pool.Fori(1, NB // 2 - 1) as j:
                pair_of_steps(j)
            pair_of_steps(NB // 2 - 1, maxima=False)
            residual(NB // 2 - 1)

            pool.wait_ge(fin_d, 6)
            nc.gpsimd.tensor_tensor(brstd[:], bvar[:], mhalf[:, 0:BATCH], ALU.pow).then_inc(fin_pool, 1)

        @block.scalar
        def _(act):
            act.dma_start(wqk[:, 0], wq_t.rearrange("(k p) o -> p k o", p=P)).then_inc(w_small, 16)
            act.dma_start(wqk[:, 1], wk_t.rearrange("(k p) o -> p k o", p=P)).then_inc(w_small, 16)
            act.dma_start(wv[:], wv_t.rearrange("(k p) o -> p k o", p=P)).then_inc(w_small, 16)
            act.dma_start(wg[:], wg_t.rearrange("(k p) e -> p k e", p=P)).then_inc(w_small, 16)

            act.wait_ge(w_small, 64)
            nc.scalar.copy(wqkh[:], wqk[:]).then_inc(wqk_split, 1)

            def m_out(e):
                for dh in range(KT):
                    act.wait_ge(m_ready, KT * e + dh + 1)
                    nc.scalar.copy(mth[:, dh, bass.ds(e, 1), :].rearrange("p o d -> p (o d)"),
                                   ps[:, M_BANK[dh], D:2 * D]).then_inc(mh_done, 1)

            def xt_out(c, k, p):
                act.wait_ge(v_ready[p], 2 * k)
                act.wait_ge(xt_stored[p], 32 * k)
                for kt in range(KT):
                    act.wait_ge(xt_psum[p], KT * k + kt + 1)
                    nc.scalar.copy(xth[:, p, kt, :], ps[:, XT_BANK[kt], :]).then_inc(xth_done, 1)
                    nc.scalar.copy(xtc[:, p, kt, :], ps[:, XT_BANK[kt], :]).then_inc(xt_evac, 1)
                act.wait_ge(xth_done, KT * (c + 1))
                act.dma_start(xth_d[:, :, bass.ds(c * CH, CH)].rearrange("k p t -> p k t"),
                              xth[:, p].bitcast(FP32)).then_inc(xt_stored[p], 16)
                act.wait_ge(xtl_done, KT * (c + 1))
                act.dma_start(xtl_d[:, :, bass.ds(c * CH, CH)].rearrange("k p t -> p k t"),
                              xtl[:, p].bitcast(FP32)).then_inc(xt_stored[p], 16)

            def qk_out(c):
                act.wait_ge(stage_out, 16 * c)
                for o in range(4):
                    act.wait_ge(qk_ready, 4 * c + o + 1)
                    nc.scalar.copy(stage[:, o, :], ps[:, QK_BANK[o], :]).then_inc(qk_evac, 1)
                act.wait_ge(qk_evac, 4 * (c + 1))
                act.dma_start(qk_d.rearrange("f (k p) t -> p (f k) t", p=P)[:, :, bass.ds(c * CH, CH)],
                              stage[:]).then_inc(stage_out, 16)

            def v_store(c):
                act.wait_ge(v_evac, 2 * (c + 1))
                act.wait_ge(ones_done, 1)
                act.dma_start(v_d[:, bass.ds(BC * c, BC)], vstage[:]).then_inc(v_stored, 16)

            m_out(0)
            xt_out(0, 0, 0)
            with act.Fori(0, NC // 2 - 1) as k:
                for p in range(2):
                    qk_out(2 * k + p)
                    xt_out(2 * k + p + 1, k + p, 1 - p)
                    v_store(2 * k + p)
                    m_out(2 * k + p + 1)
            qk_out(NC - 2)
            xt_out(NC - 1, NC // 2 - 1, 1)
            v_store(NC - 2)
            m_out(NC - 1)
            qk_out(NC - 1)
            v_store(NC - 1)

            def load_qk(c, p, gen):
                for f in range(2):
                    act.wait_ge(third_out[2 * p + f], 48 * gen)
                    for b in range(BC):
                        act.dma_start(dq[p][f][b * DH:(b + 1) * DH].rearrange("d (g t) -> d g t", t=TB),
                                      qk_d[f].rearrange("(g d) t -> d g t", d=DH)
                                      [:, :, bass.ds(c * CH + b * TB, TB)]).then_inc(dq_in[2 * p + f], 16)

            def split_qk(c, p, gen):
                for f in range(2):
                    act.wait_ge(dq_in[2 * p + f], 16 * BC * (gen + 1))
                    nc.scalar.copy(third[p][f][0], dq[p][f]).then_inc(hi_done[f], 1)
                for f in range(2):
                    act.wait_ge(r1_done[f], c + 1)
                    nc.scalar.copy(third[p][f][1], dq[p][f]).then_inc(mid_done[f], 1)
                for f in range(2):
                    act.wait_ge(mid_done[f], c + 1)
                    act.wait_ge(lo_done[f], c + 1)
                    for r in range(3):
                        act.dma_start(third_d[f, r, bass.ds(c * P, P), :], third[p][f][r]
                                      ).then_inc(third_out[2 * p + f], 16)

            act.wait_ge(stage_out, 16 * NC)
            for p in range(2):
                act.wait_ge(xn_saved[p], 16 * NC // 2)
            act.wait_ge(ml_done, KT * E)
            load_qk(0, 0, 0)
            act.wait_ge(gap_done, 1)
            nc.scalar.activation(ex[:], gap[:], ACT.Exp).then_inc(gexp_done, 1)
            with act.Fori(0, NC // 2 - 1) as k:
                load_qk(2 * k + 1, 1, k)
                split_qk(2 * k, 0, k)
                load_qk(2 * k + 2, 0, k + 1)
                split_qk(2 * k + 1, 1, k)
            load_qk(NC - 1, 1, NC // 2 - 1)
            split_qk(NC - 2, 0, NC // 2 - 1)
            split_qk(NC - 1, 1, NC // 2 - 1)

            for s in third_out:
                act.wait_ge(s, 48 * NC // 2)
            act.wait_ge(v_stored, 16 * NC)
            act.dma_start(vb[:, 0], v_d[:, 0]).then_inc(vb_in[0], 16)
            for n in range(SLOTS):
                for dst, rows, source in feature_loads(n):
                    act.dma_start(dst[rows, n, :], source).then_inc(feat_in[n], 16)

            def exps(n, kt):
                for h in range(2):
                    act.wait_ge(pv_done[kt % 4], 2 * n + kt // 4)
                    act.wait_ge(st_ready[h], NKT * n + kt + 1)
                    nc.scalar.activation(wp[:, kt % 4, h * HALF:(h + 1) * HALF], ps[:, ST_BANK[h], :],
                                         ACT.Exp).then_inc(exp_done[h], 1)

            def pv_out_at(i, u):
                n = SLOTS * i + u
                act.wait_ge(pv_done[3], 2 * n + 2)
                act.wait_ge(tr_done, 2 * i + u // 2)
                nc.scalar.copy(ot[:, :, u % 2, :], ps[:, PV_BANK, 0:4 * TB].rearrange("p (g t) -> p g t", t=TB)
                               ).then_inc(pv_evac, 1)

            def step(i, u, before=True):
                for kt in range(NKT):
                    if kt == 2 and before:
                        pv_out_at(i if u else i - 1, (u - 1) % SLOTS)
                    exps(SLOTS * i + u, kt)

            for u in range(SLOTS):
                step(0, u, before=u > 0)
            with act.Fori(1, NB // SLOTS) as i:
                for u in range(SLOTS):
                    step(i, u)
            pv_out_at(NB // SLOTS - 1, SLOTS - 1)

            act.wait_ge(fin_d, 7)
            with act.Fori(0, BATCH) as b:
                for p in range(2):
                    g = 2 * b + p
                    act.wait_ge(o_done, 2 * b)
                    nc.scalar.activation(xnc[:, p], xn[:, bass.ds(TC * g, TC), :], ACT.Identity,
                                         bias=bshift[:, bass.ds(b, 1)], scale=brstd[:, bass.ds(b, 1)]
                                         ).then_inc(z_done, 1)

        @block.vector
        def _(dve):
            nc.vector.memset(vstage[:, :, :, DH:VW], 1.0).then_inc(ones_done, 1)

            def layernorm(c, k, p):
                dve.wait_ge(x_in[p], 16 * (k + 1))
                for t in range(TC):
                    nc.vector.bn_stats(st[:, t, :], acc[:, bass.ds(TC * c + t, 1), :].rearrange("p o d -> p (o d)")
                                       ).then_inc(stats_done, 1)
                dve.wait_ge(stats_done, TC * (c + 1))
                nc.vector.tensor_tensor(part[:, 0], st[:, :, 1], st[:, :, 4], ALU.add).then_inc(part_done, 1)
                nc.vector.tensor_tensor(part[:, 1], st[:, :, 1], st[:, :, 4], ALU.subtract).then_inc(part_done, 1)
                nc.vector.tensor_tensor(part[:, 2], st[:, :, 2], st[:, :, 5], ALU.add).then_inc(part_done, 1)
                dve.wait_ge(part_done, 4 * c + 3)
                nc.vector.tensor_scalar(mean[:], part[:, 0], 0.5, None, ALU.mult).then_inc(mv_done, 1)
                nc.vector.scalar_tensor_tensor(out=part[:, 3], in0=part[:, 1], scalar=0.25, in1=part[:, 1],
                                               op0=ALU.mult, op1=ALU.mult).then_inc(part_done, 1)
                dve.wait_ge(part_done, 4 * c + 4)
                nc.vector.scalar_tensor_tensor(out=var[:], in0=part[:, 2], scalar=1.0 / D, in1=part[:, 3],
                                               op0=ALU.mult, op1=ALU.add).then_inc(mv_done, 1)
                dve.wait_ge(rstd_done, c + 1)
                dve.wait_ge(xt_psum[p], KT * k)
                dve.wait_ge(xn_saved[p], 16 * k)
                for t in range(TC):
                    nc.vector.tensor_scalar(xnc[:, p, t, :], acc[:, bass.ds(TC * c + t, 1), :].rearrange("p o d -> p (o d)"),
                                            mean[:, t:t + 1], rstd[:, t:t + 1], ALU.subtract, ALU.mult).then_inc(xn_done, 1)
                dve.wait_ge(xn_done, TC * (c + 1))

            def logits_out(c):
                dve.wait_ge(lg_ready, c + 1)
                nc.vector.tensor_copy(lg[:, bass.ds(TC * c, TC), :],
                                      ps[:, G_BANK, 0:TC * E].rearrange("p (t e) -> p t e", e=E)).then_inc(lg_evac, 1)

            def v_out(c, k, p):
                dve.wait_ge(v_stored, 16 * c)
                for h in range(2):
                    dve.wait_ge(v_ready[p], 2 * k + h + 1)
                    nc.vector.tensor_copy(vstage[:, 4 * h:4 * h + 4, :, 0:DH],
                                          ps[:, V_BANK[h], :].rearrange("p (b k d) -> p b k d", b=4, k=NKT)
                                          ).then_inc(v_evac, 1)

            def lo_halves(c, k, p):
                dve.wait_ge(v_ready[p], 2 * k)
                dve.wait_ge(xt_stored[p], 32 * k)
                for kt in range(KT):
                    dve.wait_ge(xt_evac, KT * c + kt + 1)
                    nc.vector.tensor_tensor(xtl[:, p, kt, :], ps[:, XT_BANK[kt], :],
                                            xth[:, p, kt, :].bitcast(FP32), ALU.subtract).then_inc(xtl_done, 1)

            def m_lo(e):
                for dh in range(KT):
                    dve.wait_ge(mh_done, KT * e + dh + 1)
                    nc.vector.tensor_tensor(mtl[:, dh, bass.ds(e, 1), :].rearrange("p o d -> p (o d)"),
                                            ps[:, M_BANK[dh], D:2 * D],
                                            mth[:, dh, bass.ds(e, 1), :].rearrange("p o d -> p (o d)").bitcast(FP32),
                                            ALU.subtract).then_inc(ml_done, 1)

            dve.wait_ge(wqk_split, 1)
            nc.vector.tensor_tensor(wqkl[:], wqk[:], wqkh[:].bitcast(FP32), ALU.subtract).then_inc(wqk_split, 1)
            nc.vector.memset(kf[FR:SR, :, :], 1.0).then_inc(att_const, 1)
            nc.vector.memset(mpart[:], 0.0).then_inc(att_const, 1)
            layernorm(0, 0, 0)
            m_lo(0)
            lo_halves(0, 0, 0)
            with dve.Fori(0, NC // 2 - 1) as k:
                for p in range(2):
                    layernorm(2 * k + p + 1, k + p, 1 - p)
                    lo_halves(2 * k + p + 1, k + p, 1 - p)
                    logits_out(2 * k + p)
                    v_out(2 * k + p, k, p)
                    m_lo(2 * k + p + 1)
            layernorm(NC - 1, NC // 2 - 1, 1)
            lo_halves(NC - 1, NC // 2 - 1, 1)
            logits_out(NC - 2)
            v_out(NC - 2, NC // 2 - 1, 0)
            m_lo(NC - 1)
            logits_out(NC - 1)
            v_out(NC - 1, NC // 2 - 1, 1)

            steps = [0]

            def g(instruction):
                instruction.then_inc(gate_step, 1)
                steps[0] += 1
                dve.wait_ge(gate_step, steps[0])

            def wide(a):
                return a[:].unsqueeze(2).to_broadcast([P, NT, E])

            dve.wait_ge(lg_evac, NC)
            dve.wait_ge(const_step, 6 + E)

            def pick(logits, top, onehot):
                g(nc.vector.reduce_max(top[:], logits[:], AX.X))
                g(nc.vector.tensor_tensor(eq[:], logits[:], wide(top), ALU.is_equal))
                g(nc.vector.tensor_tensor(eq[:], eq[:], rank[:].unsqueeze(1).to_broadcast([P, NT, E]), ALU.mult))
                g(nc.vector.reduce_max(first[:], eq[:], AX.X))
                g(nc.vector.tensor_tensor(onehot[:], eq[:], wide(first), ALU.is_equal))

            pick(lg, top1, oh1)
            g(nc.vector.scalar_tensor_tensor(out=lm[:], in0=oh1[:], scalar=-BIG, in1=lg[:], op0=ALU.mult, op1=ALU.add))
            pick(lm, top2, oh2)
            nc.vector.tensor_tensor(gap[:], top2[:], top1[:], ALU.subtract).then_inc(gap_done, 1)
            dve.wait_ge(gexp_done, 1)
            g(nc.vector.tensor_scalar(gs[:], ex[:], 1.0, None, ALU.add))
            g(nc.vector.reciprocal(g1[:], gs[:]))
            g(nc.vector.tensor_tensor(g2[:], ex[:], g1[:], ALU.mult))
            g(nc.vector.tensor_tensor(lm[:], oh1[:], wide(g1), ALU.mult))
            g(nc.vector.tensor_tensor(eq[:], oh2[:], wide(g2), ALU.mult))
            nc.vector.tensor_tensor(gates[:], lm[:], eq[:], ALU.add).then_inc(gates_done, 1)

            dve.wait_ge(gates_done, 1)
            with dve.Fori(0, NT // 2) as k:
                for p in range(2):
                    tile = acc[:, bass.ds(2 * k + p, 1), :].rearrange("p o d -> p (o d)")
                    for e in range(E):
                        if e % 2 == 0:
                            dve.wait_ge(y_ready[p], 4 * k + e // 2 + 1)
                        dve.wait_ge(ff_step[p], E * k + e)
                        nc.vector.scalar_tensor_tensor(
                            out=tile, in0=ps[:, 4 * p + e // 2, (e % 2) * D:(e % 2 + 1) * D],
                            scalar=gates[:, bass.ds(2 * k + p, 1), e:e + 1].rearrange("p o e -> p (o e)"),
                            in1=tile, op0=ALU.mult, op1=ALU.add).then_inc(ff_step[p], 1)

            dve.wait_ge(ff_step[1], E * NT // 2)
            nc.vector.memset(ps[:, PV_BANK, :], 0.0).then_inc(att_const, 1)

            def maxima(nth, slot_gen, par, qt):
                if qt == 0 and slot_gen is not None:
                    dve.wait_ge(msplit, slot_gen)
                dve.wait_ge(max_ready[qt % 2], 4 * nth + qt // 2 + 1)
                b = MAX_BANK[qt % 2]
                nc.vector.tensor_reduce(negm[:, par, qt:qt + 1], ps[:, b:b + 2, :].rearrange("p b c -> p (b c)"),
                                        AX.X, ALU.max, negate=True).then_inc(max_done[qt % 2], 1)

            def max_transpose(nth, par, gen):
                dve.wait_ge(msplit, 4 * (nth + 1))
                dve.wait_ge(mrow_out[par], 16 * gen)
                nc.vector.transpose(mt32[:, par], mpart[:, par]).then_inc(mt_done, 1)

            o = ps[:, TR_BANK, :].rearrange("p (g c v) -> p g c v", g=4, c=4)

            def denominators(pair):
                dve.wait_ge(tr_done, pair + 1)
                nc.vector.reciprocal(rden[:], o[:, :, :, DH]).then_inc(rden_done, 1)

            def normalise(pair):
                dve.wait_ge(rden_done, pair + 1)
                dve.wait_ge(y_done, pair)
                nc.vector.tensor_tensor(att[:].rearrange("p (c g d) -> p g c d", c=4, g=4), o[:, :, :, 0:DH],
                                        rden[:].unsqueeze(3).to_broadcast([P, 4, 4, DH]), ALU.mult
                                        ).then_inc(norm_done, 1)

            def statistics(pair):
                dve.wait_ge(y_done, pair + 1)
                nc.vector.bn_stats(ystat[:, bass.ds(pair, 1), :].rearrange("p o s -> p (o s)"),
                                   xn[:, bass.ds(pair, 1), :].rearrange("p o d -> p (o d)")).then_inc(ystat_done, 1)

            def step(i, u, pair=None, has_max=True, has_rows=True):
                n = SLOTS * i + u
                for qt in range(NKT):
                    if has_max:
                        maxima(n + 2, 4 * (n + 1), u % 2, qt)
                    if qt == 1 and has_rows:
                        max_transpose(n + 1, (u + 1) % 2, 2 * i + (u + 1) // 2)
                    if pair is not None and u % 2 == 0 and qt == 3:
                        denominators(pair)
                    if pair is not None and u % 2 == 0 and qt == 5:
                        normalise(pair)
                    if pair is not None and u % 2 == 1 and qt == 3:
                        statistics(pair)

            dve.wait_ge(att_const, 3)
            for n in range(2):
                for qt in range(NKT):
                    maxima(n, None, n, qt)
                if n == 0:
                    max_transpose(0, 0, 0)
            for u in range(SLOTS):
                step(0, u, pair=0 if u >= 2 else None)
            with dve.Fori(1, NB // SLOTS - 1) as i:
                for u in range(SLOTS):
                    step(i, u, pair=2 * i + u // 2 - 1)
            last = NB // SLOTS - 1
            for u in range(SLOTS):
                step(last, u, pair=2 * last + u // 2 - 1, has_max=u < 2, has_rows=u < 3)
            denominators(NB // 2 - 1)
            normalise(NB // 2 - 1)
            statistics(NB // 2 - 1)

            dve.wait_ge(ystat_done, NT)
            for b in range(BATCH):
                last_aggr = nc.vector.bn_aggr(bmv[:, b, :], ystat[:, b * TPB:(b + 1) * TPB, :].rearrange("p t s -> p (t s)"))
            last_aggr.then_inc(fin_d, 1)
            dve.wait_ge(fin_pe, 1)
            nc.vector.tensor_copy(bmean[:], ps[:, 0, 0:2 * BATCH].rearrange("p (b s) -> p b s", s=2)).then_inc(fin_d, 1)
            dve.wait_ge(fin_d, 2)
            nc.vector.tensor_tensor(dev2[:], bmv[:, :, 0], bmean[:, :, 0], ALU.subtract).then_inc(fin_d, 1)
            dve.wait_ge(fin_d, 3)
            nc.vector.tensor_tensor(dev2[:], dev2[:], dev2[:], ALU.mult).then_inc(fin_d, 1)
            dve.wait_ge(fin_pe, 2)
            nc.vector.tensor_tensor(bvar[:], bmean[:, :, 1], ps[:, 1, 0:BATCH], ALU.add).then_inc(fin_d, 1)
            dve.wait_ge(fin_d, 5)
            nc.vector.tensor_scalar(bvar[:], bvar[:], EPS, None, ALU.add).then_inc(fin_d, 1)
            dve.wait_ge(fin_pool, 1)
            nc.vector.scalar_tensor_tensor(out=bshift[:], in0=bmean[:, :, 0], scalar=-1.0, in1=brstd[:],
                                           op0=ALU.mult, op1=ALU.mult).then_inc(fin_d, 1)
            with dve.Fori(0, NC // 2) as k:
                for p in range(2):
                    dve.wait_ge(z_done, 2 * k + p + 1)
                    dve.wait_ge(o_out[p], 16 * k)
                    nc.vector.tensor_tensor(xtc[:, p].rearrange("p k (t d) -> p (k t) d", d=D), xnc[:, p],
                                            acc[:, bass.ds(TC * (2 * k + p), TC), :], ALU.add).then_inc(o_done, 1)

        @block.tensor
        def _(pe):
            def transposes(c, k, p):
                pe.wait_ge(xn_done, TC * (c + 1))
                pe.wait_ge(xtl_done, KT * c)
                for kt in range(KT):
                    for t in range(TC):
                        last = nc.tensor.transpose(ps[:, XT_BANK[kt], t * P:(t + 1) * P],
                                                   xnc[:, p, t, kt * P:(kt + 1) * P], ident[:])
                    last.then_inc(xt_psum[p], 1)

            def project_qk(c, p):
                pe.wait_ge(xtl_done, KT * (c + 1))
                for o in range(4):
                    pe.wait_ge(qk_evac, 4 * c + o - 1 if o > 1 else 4 * c)
                    products = [(w, v, kt) for w, v in ((wqkh, xth), (wqkh, xtl), (wqkl, xth)) for kt in range(KT)]
                    for i, (w, v, kt) in enumerate(products):
                        last = nc.tensor.matmul(ps[:, QK_BANK[o], :], w[:, o // 2, kt, (o % 2) * P:(o % 2 + 1) * P],
                                                v[:, p, kt, :], start=i == 0, stop=i == len(products) - 1)
                    last.then_inc(qk_ready, 1)

            def project_v(c, p):
                pe.wait_ge(v_evac, 2 * c)
                for h in range(2):
                    for b in range(4):
                        for par in range(2):
                            for kt in range(KT):
                                w = wv[:, kt, :].rearrange("p (g o d) -> p o g d", o=2, d=DH)[:, par]
                                last = nc.tensor.matmul(
                                    ps[par * TB:(par + 1) * TB, V_BANK[h], b * P:(b + 1) * P],
                                    xtc[:, p, kt, (4 * h + b) * TB:(4 * h + b + 1) * TB], w,
                                    start=kt == 0, stop=kt == KT - 1, tile_position=(0, par * TB))
                    last.then_inc(v_ready[p], 1)

            def logits(c, p):
                pe.wait_ge(xt_evac, KT * (c + 1))
                pe.wait_ge(lg_evac, c)
                pe.wait_ge(ml_done, KT * (c + 1))
                for t in range(TC):
                    for kt in range(KT):
                        last = nc.tensor.matmul(ps[:, G_BANK, t * E:(t + 1) * E], xtc[:, p, kt, t * P:(t + 1) * P],
                                                wg[:, kt, :], start=kt == 0, stop=kt == KT - 1)
                last.then_inc(lg_ready, 1)

            def expert_product(e):
                pe.wait_ge(ml_done, KT * e)
                pe.wait_ge(lg_evac, e)
                for s in range(2):
                    pe.wait_ge(w_in_s[s], 32 * (e + 1))
                    for dh in range(KT):
                        for h in range(HU):
                            last = nc.tensor.matmul(ps[:, M_BANK[dh], D:2 * D], win[s][:, h, dh * P:(dh + 1) * P],
                                                    wout[s][:, h, :], start=s == 0 and h == 0,
                                                    stop=s == 1 and h == HU - 1)
                        if s == 1:
                            last.then_inc(m_ready, 1)
                        elif dh == KT - 1:
                            last.then_inc(first_half, 1)

            expert_product(0)
            pe.wait_ge(const_step, 6 + E)
            transposes(0, 0, 0)
            pe.wait_ge(w_small, 64)
            pe.wait_ge(wqk_split, 2)
            with pe.Fori(0, NC // 2 - 1) as k:
                for p in range(2):
                    c = 2 * k + p
                    project_qk(c, p)
                    transposes(c + 1, k + p, 1 - p)
                    logits(c, p)
                    project_v(c, p)
                    expert_product(c + 1)
            for p in range(2):
                c = NC - 2 + p
                project_qk(c, p)
                if p == 0:
                    transposes(c + 1, NC // 2 - 1, 1)
                logits(c, p)
                project_v(c, p)
                if p == 0:
                    expert_product(c + 1)

            pe.wait_ge(ml_done, KT * E)
            pe.wait_ge(qk_evac, 4 * NC)
            pe.wait_ge(v_evac, 2 * NC)
            pe.wait_ge(lg_evac, NC)
            with pe.Fori(0, NT // 2) as k:
                for p in range(2):
                    pe.wait_ge(xtt_in[p], 32 * (k + 1))
                    pe.wait_ge(ff_step[p], E * k)
                    for j in range(E // 2):
                        products = [(v, m, kt) for kt in range(KT) for v, m in ((xtth, mth), (xtth, mtl), (xttl, mth))]
                        for i, (v, m, kt) in enumerate(products):
                            last = nc.tensor.matmul(ps[:, 4 * p + j, :], v[:, p, kt, :],
                                                    m[:, kt, 2 * j:2 * j + 2, :].rearrange("p e d -> p (e d)"),
                                                    start=i == 0, stop=i == len(products) - 1)
                        last.then_inc(y_ready[p], 1)

            def max_scores(i, u, n, qt):
                if qt == 0:
                    pe.wait_ge(feat_in[u], 96 * (i + 1))
                pe.wait_ge(max_done[qt % 2], 4 * n + qt // 2)
                for h in range(2):
                    last = nc.tensor.matmul(ps[:, MAX_BANK[qt % 2] + h, :], qf[0:FR, u, qt * P:(qt + 1) * P],
                                            kf[0:FR, u, h * HALF:(h + 1) * HALF], start=True, stop=True)
                last.then_inc(max_ready[qt % 2], 1)

            def scores(i, u, n, kt):
                if kt == 0:
                    pe.wait_ge(mrow_in[u], 48 * (i + 1))
                for h in range(2):
                    pe.wait_ge(exp_done[h], NKT * n + kt)
                    nc.tensor.matmul(ps[:, ST_BANK[h], :], kf[0:SR, u, kt * P:(kt + 1) * P],
                                     qf[0:SR, u, h * HALF:(h + 1) * HALF], start=True, stop=True
                                     ).then_inc(st_ready[h], 1)

            def sum_values(n, par, gen, kt):
                if kt == 0:
                    pe.wait_ge(vb_in[par], 16 * (gen + 1))
                    pe.wait_ge(pv_evac, n)
                for h in range(2):
                    pe.wait_ge(exp_done[h], NKT * n + kt + 1)
                for j in range(4):
                    last = nc.tensor.matmul(ps[32 * j:32 * j + VW, PV_BANK, 0:POS // 4], vb[:, par, kt, :],
                                            wp[:, kt % 4, j * (POS // 4):(j + 1) * (POS // 4)],
                                            start=kt == 0, stop=kt == NKT - 1, tile_position=(0, 32 * j))
                last.then_inc(pv_done[kt % 4], 1)

            def to_token_rows(pair):
                pe.wait_ge(pv_evac, 2 * pair + 2)
                pe.wait_ge(norm_done, pair)
                for g in range(4):
                    last = nc.tensor.transpose(ps[:, TR_BANK, g * P:(g + 1) * P],
                                               ot[:, g].rearrange("p b t -> p (b t)"), ident[:])
                last.then_inc(tr_done, 1)

            def step(i, u, pair=None, before=True, has_max=True):
                n = SLOTS * i + u
                for kt in range(0, NKT, 2):
                    scores(i, u, n, kt)
                    if has_max:
                        for t in (kt, kt + 1):
                            max_scores(i + (u + 2) // SLOTS, (u + 2) % SLOTS, n + 2, t)
                    scores(i, u, n, kt + 1)
                    for t in (kt - 2, kt - 1):
                        if kt:
                            sum_values(n, u % 2, 2 * i + u // 2, t)
                        elif before:
                            sum_values(n - 1, (u - 1) % 2, 2 * i + (u - 1) // 2, NKT + t)
                    if kt == 2 and pair is not None:
                        to_token_rows(pair)

            for p in range(2):
                pe.wait_ge(ff_step[p], E * NT // 2)
            pe.wait_ge(att_const, 2)
            for n in range(2):
                for qt in range(NKT):
                    max_scores(0, n, n, qt)
            pe.wait_ge(att_const, 3)
            for u in range(SLOTS):
                step(0, u, pair=0 if u == 2 else None, before=u > 0)
            with pe.Fori(1, NB // SLOTS - 1) as i:
                for u in range(SLOTS):
                    step(i, u, pair=2 * i + u // 2 - 1 if u % 2 == 0 else None)
            last_i = NB // SLOTS - 1
            for u in range(SLOTS):
                step(last_i, u, pair=2 * last_i + u // 2 - 1 if u % 2 == 0 else None, has_max=u < 2)
            for t in (NKT - 2, NKT - 1):
                sum_values(NB - 1, 1, NB // 2 - 1, t)
            to_token_rows(NB // 2 - 1)

            pe.wait_ge(fin_d, 1)
            nc.tensor.matmul(ps[:, 0, 0:2 * BATCH], onesm[:], bmv[:].rearrange("p b s -> p (b s)"),
                             start=True, stop=True).then_inc(fin_pe, 1)
            pe.wait_ge(fin_d, 4)
            nc.tensor.matmul(ps[:, 1, 0:BATCH], onesm[:], dev2[:], start=True, stop=True).then_inc(fin_pe, 1)


def build(nc, arrays, out_shape):
    args = [nc.dram_tensor(name, a.shape, mybir.dt.from_np(a.dtype), kind="ExternalInput").ap()
            for name, a in arrays.items()]
    result = nc.dram_tensor("result", out_shape, FP32, kind="ExternalOutput").ap()
    attention_and_experts(nc, *args, result)


def kernel(L0_attn_x, L0_attn_Wq, L0_attn_Wk, L0_attn_Wv, L0_ffn_w_gate, L0_ffn_w_in, L0_ffn_w_out):
    import numpy as np
    import concourse.bacc as bacc
    from concourse.bass_utils import run_bass_kernel_spmd

    def laid_out(a, axes=None):
        a = np.asarray(a)
        return np.ascontiguousarray(a if axes is None else np.transpose(a, axes))

    arrays = {
        "x": laid_out(L0_attn_x),
        "wq_t": laid_out(L0_attn_Wq, (1, 0)),
        "wk_t": laid_out(L0_attn_Wk, (1, 0)),
        "wv_t": laid_out(L0_attn_Wv, (1, 0)),
        "wg_t": laid_out(L0_ffn_w_gate, (1, 0)),
        "w_in": laid_out(L0_ffn_w_in),
        "w_out_t": laid_out(L0_ffn_w_out, (0, 2, 1)),
    }
    nc = bacc.Bacc("TRN2", target_bir_lowering=False, num_devices=1)
    build(nc, arrays, arrays["x"].shape)
    r = run_bass_kernel_spmd(nc, [arrays], core_ids=[0])
    return r.results[0]["result"]
```

```python
import concourse.bass as bass
from concourse import mybir
from contextlib import ExitStack


FP32 = mybir.dt.float32
FP32R = mybir.dt.float32r
BF16 = mybir.dt.bfloat16
ALU = mybir.AluOpType
ACT = mybir.ActivationFunctionType
AX = mybir.AxisListType

P = 128
EPS = 1e-5
BIG = 3e38


def attention_and_experts(nc, x, wq_t, wk_t, wv_t, wg_t, w_in, w_out_t, out):
    BATCH, S, D = x.shape
    T = BATCH * S
    NT = T // P
    KT = D // P
    HEADS = 16
    DH = D // HEADS
    NB = HEADS * BATCH
    TB = T // NB
    G = D // DH
    POS = TB * G
    NKT = POS // P
    HALF = POS // 2
    TC = 4
    CH = TC * P
    NC = T // CH
    BC = CH // TB
    E, HID, _ = w_in.shape
    HU = HID // 2 // P
    VW = DH + 1
    RUNS = (3, 2, 1)
    FR = DH * sum(RUNS)
    SR = FR + 3
    SLOTS = 4
    TPB = NT // BATCH
    XS = 4
    EARLY = BATCH - 1
    Y1 = NT - NKT

    x_v = x.rearrange("a (t p) d -> p (a t) d", p=P)
    out_v = out.rearrange("a (t p) d -> p (a t) d", p=P)

    qk_d = nc.dram_tensor("qk_d", [2, KT * P, T], FP32, kind="Internal").ap()
    third_d = nc.dram_tensor("third_d", [2, 3, NB * DH, POS], BF16, kind="Internal").ap()
    xth_d = nc.dram_tensor("xth_d", [KT, P, T], FP32, kind="Internal").ap()
    xtl_d = nc.dram_tensor("xtl_d", [KT, P, T], FP32, kind="Internal").ap()
    v_d = nc.dram_tensor("v_d", [T, 2, NKT * VW], FP32, kind="Internal").ap()
    max_d = nc.dram_tensor("max_d", [2, P, 32], BF16, kind="Internal").ap()

    ctx = ExitStack()
    with ctx:
        def sb(name, shape, dt=FP32):
            return ctx.enter_context(nc.sbuf_tensor(name, shape, dt))

        def sem(name, n=None):
            if n is None:
                return ctx.enter_context(nc.semaphore(name))
            return [ctx.enter_context(nc.semaphore(f"{name}{i}")) for i in range(n)]

        acc = sb("acc", [P, NT, D])
        xn = sb("xn", [P, NT, D])
        mth = sb("mth", [P, KT, E, D], FP32R)
        mtl = sb("mtl", [P, KT, E, D], FP32R)
        wqkh = sb("wqkh", [P, 2, KT, D], FP32R)
        wqkl = sb("wqkl", [P, 2, KT, D], FP32R)
        wvgh = sb("wvgh", [P, KT, D + E], FP32R)
        wvgl = sb("wvgl", [P, KT, D + E], FP32R)
        ident = sb("ident", [P, P])
        onesm = sb("onesm", [P, P])
        xnc = sb("xnc", [P, 2, TC, D])
        xth = sb("xth", [P, 2, KT, CH], FP32R)
        xtl = sb("xtl", [P, 2, KT, CH], FP32R)
        stage = sb("stage", [P, 2 * KT, CH])
        vstage = sb("vstage", [P, TC, 2, NKT, VW])
        st = sb("st", [P, TC, 6])
        part = sb("part", [P, 4, TC])
        mean = sb("mean", [P, TC])
        var = sb("var", [P, TC])
        veps = sb("veps", [P, TC])
        rstd = sb("rstd", [P, TC])
        mhalf = sb("mhalf", [P, 8])
        epst = sb("epst", [P, 8])
        zero = sb("zero", [P, 8])
        spare = sb("spare", [P, 2, TC, D])
        wqk = spare[:, 0].rearrange("p (f k) d -> p f k d", f=2)
        wvg = spare[:, 1].rearrange("p t d -> p (t d)")[:, 0:KT * (D + E)].rearrange("p (k o) -> p k o", k=KT)
        lg = sb("lg", [P, NT, E])
        rank = sb("rank", [P, E])
        eq = sb("eq", [P, NT, E])
        oh1 = sb("oh1", [P, NT, E])
        oh2 = sb("oh2", [P, NT, E])
        lm = sb("lm", [P, NT, E])
        gates = sb("gates", [P, NT, E])
        top1 = sb("top1", [P, NT])
        top2 = sb("top2", [P, NT])
        first = sb("first", [P, NT])
        gap = sb("gap", [P, NT])
        ex = sb("ex", [P, NT])
        gs = sb("gs", [P, NT])
        g1 = sb("g1", [P, NT])
        g2 = sb("g2", [P, NT])
        xtth = sb("xtth", [P, XS, KT, P], FP32R)
        odd = sb("odd", [P, D])
        xttl = sb("xttl", [P, XS, KT, P], FP32R)
        wp = sb("wp", [P, 4, POS])
        win = [wp[:, 2 * s, :].rearrange("p (h d) -> p h d", h=HU) for s in range(2)]
        wout = [wp[:, 2 * s + 1, :].rearrange("p (h d) -> p h d", h=HU) for s in range(2)]
        dqk = [stage[:].rearrange("p k t -> p (k t)"), xnc[:].rearrange("p f t d -> p (f t d)")]
        dq = [[a[:, f * POS:(f + 1) * POS] for f in range(2)] for a in dqk]
        room = [wp[:, i, :] for i in range(4)] + [spare[:, i].rearrange("p t d -> p (t d)") for i in range(2)]
        room = [r.bitcast(BF16)[:, h * POS:(h + 1) * POS] for r in room for h in range(2)]
        third = [[room[6 * p + 3 * f:6 * p + 3 * f + 3] for f in range(2)] for p in range(2)]
        outs = [spare[:, i] for i in range(2)]
        outs += [stage[:, 2 * i:2 * i + 2].rearrange("p k (t d) -> p (k t) d", d=D) for i in range(2)]
        qf = sb("qf", [SR, SLOTS, POS], BF16)
        kf = sb("kf", [SR, SLOTS, POS], BF16)
        vb = sb("vb", [P, 2, NKT, VW])
        negm = sb("negm", [P, 2, NKT])
        mrest = sb("mrest", [P, 2, NKT])
        mpart = sb("mpart", [P, 2, 32], BF16)
        mt32 = sb("mt32", [P, 2, 32], BF16)
        ot = sb("ot", [P, 4, 2, TB])
        rden = sb("rden", [P, 4, 4])
        att = sb("att", [P, D])
        ystat = sb("ystat", [P, NT, 6])
        bmv = sb("bmv", [P, BATCH, 2])
        dev2 = sb("dev2", [P, BATCH])
        bmean = sb("bmean", [P, BATCH, 2])
        bvar = sb("bvar", [P, BATCH])
        brstd = sb("brstd", [P, BATCH])
        bshift = sb("bshift", [P, BATCH])

        ps = ctx.enter_context(nc.psum_tensor("ps", [P, 8, 512], FP32))
        XT_BANK = (0, 1)
        QK_BANK = (2, 3, 2, 3)
        V_BANK = (5, 6)
        M_BANK = (4, 7)
        MAX_BANK = (0, 2)
        ST_BANK = (4, 5)
        Y_BANK = (4, 5, 6, 7)
        PV_BANK = 6
        TR_BANK = 7

        w_small = sem("w_small")
        x_in = sem("x_in", 2)
        const_step = sem("const_step")
        stats_done = sem("stats_done")
        part_done = sem("part_done")
        mv_done = sem("mv_done")
        veps_done = sem("veps_done")
        rstd_done = sem("rstd_done")
        xn_done = sem("xn_done")
        xn_saved = sem("xn_saved", 2)
        xt_psum = sem("xt_psum", 2)
        xth_done = sem("xth_done")
        xtl_done = sem("xtl_done")
        w_hi = sem("w_hi")
        w_lo = sem("w_lo")
        xt_stored = sem("xt_stored", 2)
        qk_ready = sem("qk_ready")
        qk_evac = sem("qk_evac")
        stage_out = sem("stage_out")
        v_ready = sem("v_ready", 2)
        v_evac = sem("v_evac", 2)
        ones_done = sem("ones_done")
        v_stored = sem("v_stored")
        lg_evac = sem("lg_evac", 2)
        gate_step = sem("gate_step")
        gap_done = sem("gap_done")
        gexp_done = sem("gexp_done")
        gates_done = sem("gates_done")
        dq_in = sem("dq_in", 2)
        hi_done = sem("hi_done", 2)
        r1_done = sem("r1_done", 2)
        mid_done = sem("mid_done", 2)
        lo_done = sem("lo_done", 2)
        third_out = sem("third_out", 4)
        w_in_s = sem("w_in_s", 2)
        first_half = sem("first_half")
        m_ready = sem("m_ready")
        mh_done = sem("mh_done")
        ml_done = sem("ml_done")
        xtt_in = sem("xtt_in", XS)
        y_ready = sem("y_ready", E // 2)
        ff_added = sem("ff_added", E // 2)
        ff_sum = sem("ff_sum")
        att_const = sem("att_const")
        feat_in = sem("feat_in", SLOTS)
        vb_in = sem("vb_in", 2)
        st_ready = sem("st_ready", 2)
        exp_done = sem("exp_done", 2)
        pv_done = sem("pv_done", 4)
        pv_evac = sem("pv_evac")
        max_ready = sem("max_ready", 2)
        max_done = sem("max_done", 2)
        msplit = sem("msplit")
        mt_done = sem("mt_done")
        mrow_out = sem("mrow_out", 2)
        mrow_in = sem("mrow_in", SLOTS)
        tr_done = sem("tr_done")
        rden_done = sem("rden_done")
        norm_done = sem("norm_done")
        y_done = sem("y_done")
        ystat_done = sem("ystat_done")
        fin_d = sem("fin_d")
        fin_pe = sem("fin_pe")
        fin_pool = sem("fin_pool")
        zd_done = sem("zd_done")
        z_done = sem("z_done")
        o_done = sem("o_done")
        o_out = sem("o_out", 4)

        def feature_loads(n):
            block_rows = bass.ds(n * DH, DH)
            for k_third, length in enumerate(RUNS):
                start = sum(RUNS[:k_third])
                rows = slice(start * DH, (start + length) * DH)
                yield qf, rows, third_d[0, 0:length, block_rows, :]
                yield kf, rows, third_d[1, k_third, block_rows, :].unsqueeze(0).to_broadcast([length, DH, POS])

        def value_loads(n, par):
            for o in range(2):
                yield (vb[o * TB:(o + 1) * TB, par].rearrange("p k v -> p (k v)"),
                       v_d[bass.ds(n * TB, TB), o, :])

        block = ctx.enter_context(nc.Block())

        @block.sync
        def _(sp):
            def load_x(c, k, p):
                sp.wait_ge(x_in[p], 16 * k)
                sp.dma_start(acc[:, bass.ds(TC * c, TC), :], x_v[:, bass.ds(TC * c, TC), :]).then_inc(x_in[p], 16)

            def load_weights(e, s):
                if s == 0:
                    sp.wait_ge(first_half, e)
                else:
                    sp.wait_ge(ml_done, KT * e)
                rows = bass.ds(e * HID + s * HU * P, HU * P)
                sp.dma_start(win[s], w_in.rearrange("e h d -> (e h) d")[rows, :]
                             .rearrange("(p h) d -> p h d", h=HU)).then_inc(w_in_s[s], 16)
                sp.dma_start(wout[s], w_out_t.rearrange("e h d -> (e h) d")[rows, :]
                             .rearrange("(p h) d -> p h d", h=HU)).then_inc(w_in_s[s], 16)

            load_weights(0, 0)
            load_x(0, 0, 0)
            for dst, w in ((wqk[:, 0], wq_t), (wqk[:, 1], wk_t), (wvg[:, :, 0:D], wv_t), (wvg[:, :, D:D + E], wg_t)):
                sp.dma_start(dst, w.rearrange("(k p) o -> p k o", p=P)).then_inc(w_small, 16)
            load_weights(0, 1)
            load_x(1, 0, 1)
            with sp.Fori(1, NC // 2) as k:
                load_x(2 * k, k, 0)
                for h in range(2):
                    load_weights(2 * k - 1, h)
                load_x(2 * k + 1, k, 1)
                for h in range(2):
                    load_weights(2 * k, h)

            def load_xt(t, slot):
                for half, src in ((xtth, xth_d), (xttl, xtl_d)):
                    sp.dma_start(half[:, slot].bitcast(FP32), src[:, :, bass.ds(t * P, P)]
                                 .rearrange("k p t -> p k t")).then_inc(xtt_in[slot], 16)

            def next_xt(t, slot):
                sp.wait_ge(y_ready[-1], t - XS + 1)
                load_xt(t, slot)

            sp.wait_ge(xt_stored[0], 32)
            for t in range(XS):
                load_xt(t, t)
            for h in range(2):
                load_weights(E - 1, h)
            for p in range(2):
                sp.wait_ge(xt_stored[p], 32 * NC // 2)
            with sp.Fori(1, Y1 // XS) as k:
                for slot in range(XS):
                    next_xt(XS * k + slot, slot)

            def features(n, slot):
                for dst, rows, source in feature_loads(n):
                    sp.dma_start(dst[rows, slot, :], source).then_inc(feat_in[slot], 16)

            def values(n, par):
                for dst, source in value_loads(n, par):
                    sp.dma_start(dst, source).then_inc(vb_in[par], 16)

            def max_rows(slot, par, nth, gen_in, gen_slot):
                sp.wait_ge(mt_done, nth + 1)
                sp.wait_ge(mrow_in[(slot + 2) % SLOTS], 16 * gen_in)
                sp.dma_start(max_d[par], mt32[:, par]).then_inc(mrow_out[par], 16)
                sp.wait_ge(mrow_out[par], 16 * (gen_slot + 1))
                for c in range(3):
                    sp.dma_start(qf[FR + c:FR + c + 1, slot, :].rearrange("o (t q r) -> o t q r", q=4, r=32),
                                 max_d[par].rearrange("(q c t) r -> c t q r", q=4, c=4)[c:c + 1]
                                 ).then_inc(mrow_in[slot], 16)

            for f in range(2):
                sp.wait_ge(third_out[f], 48)
            for t in range(Y1, NT):
                if t - Y1 < SLOTS:
                    features(t - Y1, t - Y1)
                next_xt(t, t % XS)
            sp.wait_ge(v_stored, 16 * NC)
            values(0, 0)
            max_rows(0, 0, 0, 0, 0)
            for s in third_out:
                sp.wait_ge(s, 48 * NC // 2)

            def step(i, u):
                n = SLOTS * i + u
                sp.wait_ge(pv_done[3], 2 * n)
                values(n + 1, (u + 1) % 2)
                m = u + 1
                max_rows(m % SLOTS, m % 2, n + 1, 3 * (i if u == 0 else i + (m - 2) // SLOTS + 1),
                         2 * i + m // 2)

            def step_features(i, u):
                for h in range(2):
                    sp.wait_ge(st_ready[h], NKT * (SLOTS * i + u + 1))
                features(SLOTS * i + u + SLOTS, u)

            with sp.Fori(0, NB // SLOTS - 1) as i:
                for u in range(SLOTS):
                    step(i, u)
                    step_features(i, u)
            for u in range(SLOTS - 1):
                step(NB // SLOTS - 1, u)

            pieces = [(c, c % 4, 0, TC) for c in range(EARLY * NC // BATCH)]
            pieces += [(c, c % 4, h * TC // 2, TC // 2) for c in range(EARLY * NC // BATCH, NC) for h in range(2)]
            for i, (c, p, t, n) in enumerate(pieces):
                sp.wait_ge(o_done, i + 1)
                sp.dma_start(out_v[:, TC * c + t:TC * c + t + n, :], outs[p][:, t:t + n]).then_inc(o_out[p], 16)
            for p in range(4):
                sp.wait_ge(o_out[p], 16 * sum(slot == p for _, slot, _, _ in pieces))

        @block.gpsimd
        def _(pool):
            nc.gpsimd.memset(ident[:], 0.0).then_inc(const_step, 1)
            nc.gpsimd.memset(onesm[:], 1.0 / P).then_inc(const_step, 1)
            for value, tile in ((-0.5, mhalf), (EPS, epst), (0.0, zero)):
                nc.gpsimd.memset(tile[:], value).then_inc(const_step, 1)
            for e in range(E):
                nc.gpsimd.memset(rank[:, e:e + 1], float(E - e)).then_inc(const_step, 1)
            pool.wait_ge(const_step, 5 + E)
            nc.gpsimd.affine_select(out=ident[:], in_=ident[:], compare_op=ALU.not_equal, fill=1.0,
                                    base=0, pattern=[[-1, P]], channel_multiplier=1).then_inc(const_step, 1)

            with pool.Fori(0, NC // 2) as k:
                for p in range(2):
                    c = 2 * k + p
                    pool.wait_ge(mv_done, 2 * (c + 1))
                    nc.gpsimd.tensor_tensor(veps[:], var[:], epst[:, 0:TC], ALU.add).then_inc(veps_done, 1)
                    pool.wait_ge(veps_done, c + 1)
                    nc.gpsimd.tensor_tensor(rstd[:], veps[:], mhalf[:, 0:TC], ALU.pow).then_inc(rstd_done, 1)
                    pool.wait_ge(xn_done, TC * (c + 1))
                    nc.gpsimd.tensor_tensor(xn[:, bass.ds(TC * c, TC), :], xnc[:, p],
                                            zero[:, 0:TC].unsqueeze(2).to_broadcast([P, TC, D]),
                                            ALU.add).then_inc(xn_saved[p], 1)

            with pool.Fori(0, NC // 2) as k:
                for p in range(2):
                    for f in range(2):
                        pool.wait_ge(hi_done[f], 2 * k + p + 1)
                        nc.gpsimd.tensor_tensor(dq[p][f], dq[p][f], third[p][f][0], ALU.subtract).then_inc(r1_done[f], 1)
                    for f in range(2):
                        pool.wait_ge(mid_done[f], 2 * k + p + 1)
                        nc.gpsimd.tensor_tensor(third[p][f][2], dq[p][f], third[p][f][1],
                                                ALU.subtract).then_inc(lo_done[f], 1)

            def max_thirds(nth, par, first=False):
                for s in range(2):
                    pool.wait_ge(max_done[s], 4 * (nth + 1))
                if not first:
                    pool.wait_ge(mt_done, nth - 1)
                c0, c1, c2 = (mpart[:, par, 8 * c:8 * c + 8] for c in range(3))
                nc.gpsimd.tensor_tensor(c0, negm[:, par], zero[:], ALU.add).then_inc(msplit, 1)
                pool.wait_ge(msplit, 4 * nth + 1)
                nc.gpsimd.tensor_tensor(mrest[:, par], negm[:, par], c0, ALU.subtract).then_inc(msplit, 1)
                pool.wait_ge(msplit, 4 * nth + 2)
                nc.gpsimd.tensor_tensor(c1, mrest[:, par], zero[:], ALU.add).then_inc(msplit, 1)
                pool.wait_ge(msplit, 4 * nth + 3)
                nc.gpsimd.tensor_tensor(c2, mrest[:, par], c1, ALU.subtract).then_inc(msplit, 1)

            def residual(pair):
                pool.wait_ge(norm_done, pair + 1)
                nc.gpsimd.tensor_tensor(xn[:, bass.ds(pair, 1), :].rearrange("p o d -> p (o d)"),
                                        xn[:, bass.ds(pair, 1), :].rearrange("p o d -> p (o d)"),
                                        att[:], ALU.add).then_inc(y_done, 1)

            for p in range(2):
                pool.wait_ge(xn_saved[p], NC // 2)
            max_thirds(0, 0, first=True)
            max_thirds(1, 1, first=True)

            def pair_of_steps(j, residuals=True, maxima=True):
                if residuals:
                    residual(j - 1)
                if maxima:
                    max_thirds(2 * j + 2, 0)
                    max_thirds(2 * j + 3, 1)

            pair_of_steps(0, residuals=False)
            with pool.Fori(1, NB // 2 - 1) as j:
                pair_of_steps(j)
            pair_of_steps(NB // 2 - 1, maxima=False)
            def batch_rstd(part, entries):
                pool.wait_ge(fin_d, 7 * part + 6)
                nc.gpsimd.tensor_tensor(brstd[:, entries], bvar[:, entries],
                                        mhalf[:, 0:entries.stop - entries.start], ALU.pow).then_inc(fin_pool, 1)

            batch_rstd(0, slice(0, EARLY))
            residual(NB // 2 - 1)
            batch_rstd(1, slice(EARLY, BATCH))

        @block.scalar
        def _(act):
            act.wait_ge(w_small, 64)
            nc.scalar.copy(wqkh[:], wqk).then_inc(w_hi, 1)
            nc.scalar.copy(wvgh[:], wvg).then_inc(w_hi, 1)

            def m_out(e):
                for dh in range(KT):
                    act.wait_ge(m_ready, KT * e + dh + 1)
                    nc.scalar.copy(mth[:, dh, bass.ds(e, 1), :].rearrange("p o d -> p (o d)"),
                                   ps[:, M_BANK[dh], 0:D]).then_inc(mh_done, 1)

            def xt_out(c, k, p, first=False):
                if not first:
                    act.wait_ge(v_ready[1], 2 * (c - 1))
                act.wait_ge(xt_stored[p], 32 * k)
                for kt in range(KT):
                    act.wait_ge(xt_psum[p], KT * k + kt + 1)
                    nc.scalar.copy(xth[:, p, kt, :], ps[:, XT_BANK[kt], :]).then_inc(xth_done, 1)

            def xt_store(c, p):
                for done, half, dst in ((xth_done, xth, xth_d), (xtl_done, xtl, xtl_d)):
                    act.wait_ge(done, KT * (c + 1))
                    act.dma_start(dst[:, :, bass.ds(c * CH, CH)].rearrange("k p t -> p k t"),
                                  half[:, p].bitcast(FP32)).then_inc(xt_stored[p], 16)

            def qk_out(c):
                act.wait_ge(stage_out, 16 * c)
                for o in range(4):
                    act.wait_ge(qk_ready, 4 * c + o + 1)
                    nc.scalar.copy(stage[:, o, :], ps[:, QK_BANK[o], :]).then_inc(qk_evac, 1)
                act.wait_ge(qk_evac, 4 * (c + 1))
                act.dma_start(qk_d.rearrange("f (k p) t -> p (f k) t", p=P)[:, :, bass.ds(c * CH, CH)],
                              stage[:]).then_inc(stage_out, 16)

            def v_out(c, t):
                if t == 0:
                    act.wait_ge(v_stored, 16 * c)
                act.wait_ge(v_ready[t % 2], 2 * c + t // 2 + 1)
                nc.scalar.copy(lg[:, bass.ds(TC * c + t, 1), :].rearrange("p o e -> p (o e)"),
                               ps[:, V_BANK[t % 2], D:D + E]).then_inc(lg_evac[t % 2], 1)
                nc.scalar.copy(vstage[:, t, :, :, 0:DH], ps[:, V_BANK[t % 2], 0:D]
                               .rearrange("p (k o d) -> p o k d", o=2, d=DH)).then_inc(v_evac[t % 2], 1)

            def v_store(c):
                for h in range(2):
                    act.wait_ge(v_evac[h], 2 * (c + 1))
                act.wait_ge(ones_done, 1)
                act.dma_start(v_d[bass.ds(c * CH, CH)].rearrange("(t p) o f -> p t (o f)", p=P),
                              vstage[:].rearrange("p t o k v -> p t (o k v)")).then_inc(v_stored, 16)

            def chunk(c, following=None):
                qk_out(c)
                v_out(c, 0)
                v_out(c, 1)
                if following:
                    xt_out(c + 1, *following)
                v_out(c, 2)
                v_out(c, 3)
                v_store(c)
                if following:
                    xt_store(c + 1, following[1])
                    m_out(c + 1)

            xt_out(0, 0, 0, first=True)
            m_out(0)
            xt_store(0, 0)
            with act.Fori(0, NC // 2 - 1) as k:
                for p in range(2):
                    chunk(2 * k + p, (k + p, 1 - p))
            chunk(NC - 2, (NC // 2 - 1, 1))
            chunk(NC - 1)

            def load_qk(c, p, gen):
                for f in range(2):
                    act.wait_ge(third_out[2 * p + f], 48 * gen)
                for b in range(BC):
                    act.dma_start(dqk[p][b * DH:(b + 1) * DH].rearrange("d (g t) -> d g t", t=TB),
                                  qk_d.rearrange("f (g d) t -> d (f g) t", d=DH)
                                  [:, :, bass.ds(c * CH + b * TB, TB)]).then_inc(dq_in[p], 16)

            def split_qk(c, p, gen):
                act.wait_ge(dq_in[p], 16 * BC * (gen + 1))
                for f in range(2):
                    nc.scalar.copy(third[p][f][0], dq[p][f]).then_inc(hi_done[f], 1)
                for f in range(2):
                    act.wait_ge(r1_done[f], c + 1)
                    nc.scalar.copy(third[p][f][1], dq[p][f]).then_inc(mid_done[f], 1)
                for f in range(2):
                    act.wait_ge(mid_done[f], c + 1)
                    act.wait_ge(lo_done[f], c + 1)
                    for r in range(3):
                        act.dma_start(third_d[f, r, bass.ds(c * P, P), :], third[p][f][r]
                                      ).then_inc(third_out[2 * p + f], 16)

            act.wait_ge(gap_done, 1)
            nc.scalar.activation(ex[:], gap[:], ACT.Exp).then_inc(gexp_done, 1)
            act.wait_ge(stage_out, 16 * NC)
            for p in range(2):
                act.wait_ge(xn_saved[p], NC // 2)
            act.wait_ge(ml_done, KT * E)
            load_qk(0, 0, 0)
            with act.Fori(0, NC // 2 - 1) as k:
                load_qk(2 * k + 1, 1, k)
                split_qk(2 * k, 0, k)
                load_qk(2 * k + 2, 0, k + 1)
                split_qk(2 * k + 1, 1, k)
            load_qk(NC - 1, 1, NC // 2 - 1)
            split_qk(NC - 2, 0, NC // 2 - 1)
            split_qk(NC - 1, 1, NC // 2 - 1)

            for s in third_out:
                act.wait_ge(s, 48 * NC // 2)

            def exps(n, kt):
                for h in range(2):
                    act.wait_ge(pv_done[kt % 4], 2 * n + kt // 4)
                    act.wait_ge(st_ready[h], NKT * n + kt + 1)
                    nc.scalar.activation(wp[:, kt % 4, h * HALF:(h + 1) * HALF], ps[:, ST_BANK[h], :],
                                         ACT.Exp).then_inc(exp_done[h], 1)

            def pv_out_at(i, u):
                n = SLOTS * i + u
                act.wait_ge(pv_done[3], 2 * n + 2)
                act.wait_ge(tr_done, 2 * i + u // 2)
                nc.scalar.copy(ot[:, :, u % 2, :], ps[:, PV_BANK, 0:4 * TB].rearrange("p (g t) -> p g t", t=TB)
                               ).then_inc(pv_evac, 1)

            def step(i, u, before=True):
                for kt in range(NKT):
                    exps(SLOTS * i + u, kt)
                    if kt == 2 and before:
                        pv_out_at(i if u else i - 1, (u - 1) % SLOTS)

            for u in range(SLOTS):
                step(0, u, before=u > 0)
            with act.Fori(1, NB // SLOTS) as i:
                for u in range(SLOTS):
                    step(i, u)
            pv_out_at(NB // SLOTS - 1, SLOTS - 1)

            act.wait_ge(fin_d, 14)
            for p in range(2):
                act.wait_ge(o_done, EARLY * NC // BATCH)
                first_tile = EARLY * TPB + TC * p
                for h in range(2):
                    t = slice(h * TC // 2, (h + 1) * TC // 2)
                    nc.scalar.activation(xnc[:, p, t], xn[:, first_tile + t.start:first_tile + t.stop, :], ACT.Identity,
                                         bias=bshift[:, EARLY:BATCH], scale=brstd[:, EARLY:BATCH]).then_inc(z_done, 1)

        @block.vector
        def _(dve):
            nc.vector.memset(vstage[:, :, :, :, DH:VW], 1.0).then_inc(ones_done, 1)
            nc.vector.memset(kf[FR:SR, :, :], 1.0).then_inc(att_const, 1)
            nc.vector.memset(mpart[:], 0.0).then_inc(att_const, 1)

            def layernorm(c, k, p):
                dve.wait_ge(x_in[p], 16 * (k + 1))
                for t in range(TC):
                    nc.vector.bn_stats(st[:, t, :], acc[:, bass.ds(TC * c + t, 1), :].rearrange("p o d -> p (o d)")
                                       ).then_inc(stats_done, 1)
                dve.wait_ge(stats_done, TC * (c + 1))
                nc.vector.tensor_tensor(part[:, 0], st[:, :, 1], st[:, :, 4], ALU.add).then_inc(part_done, 1)
                nc.vector.tensor_tensor(part[:, 1], st[:, :, 1], st[:, :, 4], ALU.subtract).then_inc(part_done, 1)
                nc.vector.tensor_tensor(part[:, 2], st[:, :, 2], st[:, :, 5], ALU.add).then_inc(part_done, 1)
                dve.wait_ge(part_done, 4 * c + 3)
                nc.vector.tensor_scalar(mean[:], part[:, 0], 0.5, None, ALU.mult).then_inc(mv_done, 1)
                nc.vector.scalar_tensor_tensor(out=part[:, 3], in0=part[:, 1], scalar=0.25, in1=part[:, 1],
                                               op0=ALU.mult, op1=ALU.mult).then_inc(part_done, 1)
                dve.wait_ge(part_done, 4 * c + 4)
                nc.vector.scalar_tensor_tensor(out=var[:], in0=part[:, 2], scalar=1.0 / D, in1=part[:, 3],
                                               op0=ALU.mult, op1=ALU.add).then_inc(mv_done, 1)
                dve.wait_ge(rstd_done, c + 1)
                dve.wait_ge(xt_psum[p], KT * k)
                dve.wait_ge(xn_saved[p], k)
                for t in range(TC):
                    nc.vector.tensor_scalar(xnc[:, p, t, :], acc[:, bass.ds(TC * c + t, 1), :].rearrange("p o d -> p (o d)"),
                                            mean[:, t:t + 1], rstd[:, t:t + 1], ALU.subtract, ALU.mult).then_inc(xn_done, 1)
                dve.wait_ge(xn_done, TC * (c + 1))

            def lo_halves(c, k, p, first=False):
                if not first:
                    dve.wait_ge(v_ready[1], 2 * (c - 1))
                dve.wait_ge(xt_stored[p], 32 * k)
                for kt in range(KT):
                    dve.wait_ge(xth_done, KT * c + kt + 1)
                    nc.vector.tensor_tensor(xtl[:, p, kt, :], ps[:, XT_BANK[kt], :],
                                            xth[:, p, kt, :].bitcast(FP32), ALU.subtract).then_inc(xtl_done, 1)

            def m_lo(e):
                for dh in range(KT):
                    dve.wait_ge(mh_done, KT * e + dh + 1)
                    nc.vector.tensor_tensor(mtl[:, dh, bass.ds(e, 1), :].rearrange("p o d -> p (o d)"),
                                            ps[:, M_BANK[dh], 0:D],
                                            mth[:, dh, bass.ds(e, 1), :].rearrange("p o d -> p (o d)").bitcast(FP32),
                                            ALU.subtract).then_inc(ml_done, 1)

            def chunk(c, following, second=None):
                lo_halves(c + 1, *following)
                if second:
                    layernorm(c + 2, *second)
                m_lo(c + 1)

            layernorm(0, 0, 0)
            dve.wait_ge(w_hi, 2)
            nc.vector.tensor_tensor(wqkl[:], wqk, wqkh[:].bitcast(FP32), ALU.subtract).then_inc(w_lo, 1)
            nc.vector.tensor_tensor(wvgl[:], wvg, wvgh[:].bitcast(FP32), ALU.subtract).then_inc(w_lo, 1)
            lo_halves(0, 0, 0, first=True)
            layernorm(1, 0, 1)
            m_lo(0)
            with dve.Fori(0, NC // 2 - 1) as k:
                for p in range(2):
                    chunk(2 * k + p, (k + p, 1 - p), (k + 1, p))
            chunk(NC - 2, (NC // 2 - 1, 1))

            steps = [0]

            def g(instruction):
                instruction.then_inc(gate_step, 1)
                steps[0] += 1
                dve.wait_ge(gate_step, steps[0])

            def wide(a):
                return a.unsqueeze(2).to_broadcast([P, a.shape[1], E])

            dve.wait_ge(const_step, 6 + E)

            def pick(rows, logits, top, onehot):
                n = rows.stop - rows.start

                g(nc.vector.reduce_max(top[:, rows], logits[:, rows], AX.X))
                g(nc.vector.tensor_tensor(eq[:, rows], logits[:, rows], wide(top[:, rows]), ALU.is_equal))
                g(nc.vector.tensor_tensor(eq[:, rows], eq[:, rows], rank[:].unsqueeze(1).to_broadcast([P, n, E]), ALU.mult))
                g(nc.vector.reduce_max(first[:, rows], eq[:, rows], AX.X))
                g(nc.vector.tensor_tensor(onehot[:, rows], eq[:, rows], wide(first[:, rows]), ALU.is_equal))

            for chunks, rows in ((NC - 1, slice(0, NT - TC)), (NC, slice(NT - TC, NT))):
                for h in range(2):
                    dve.wait_ge(lg_evac[h], 2 * chunks)
                pick(rows, lg, top1, oh1)
                g(nc.vector.scalar_tensor_tensor(out=lm[:, rows], in0=oh1[:, rows], scalar=-BIG, in1=lg[:, rows],
                                                 op0=ALU.mult, op1=ALU.add))
                pick(rows, lm, top2, oh2)
            nc.vector.tensor_tensor(gap[:], top2[:], top1[:], ALU.subtract).then_inc(gap_done, 1)
            dve.wait_ge(gexp_done, 1)
            g(nc.vector.tensor_scalar(gs[:], ex[:], 1.0, None, ALU.add))
            g(nc.vector.reciprocal(g1[:], gs[:]))
            g(nc.vector.tensor_tensor(g2[:], ex[:], g1[:], ALU.mult))
            g(nc.vector.tensor_tensor(lm[:], oh1[:], wide(g1[:]), ALU.mult))
            g(nc.vector.tensor_tensor(eq[:], oh2[:], wide(g2[:]), ALU.mult))
            nc.vector.tensor_tensor(gates[:], lm[:], eq[:], ALU.add).then_inc(gates_done, 1)

            dve.wait_ge(gates_done, 1)

            def add_experts(t, banks):
                tile = acc[:, bass.ds(t, 1), :].rearrange("p o d -> p (o d)")
                for j in banks:
                    dve.wait_ge(y_ready[j], t + 1)
                    for h, total in enumerate((tile, odd[:])):
                        product = ps[:, Y_BANK[j], h * D:(h + 1) * D]
                        gate = gates[:, bass.ds(t, 1), 2 * j + h:2 * j + h + 1].rearrange("p o e -> p (o e)")
                        if j:
                            dve.wait_ge(ff_added[j - 1], 2 * t + h + 1)
                        if j == 0 and h == 1:
                            dve.wait_ge(ff_sum, t)
                            nc.vector.tensor_scalar(total, product, gate, None, ALU.mult).then_inc(ff_added[j], 1)
                        else:
                            nc.vector.scalar_tensor_tensor(out=total, in0=product, scalar=gate, in1=total,
                                                           op0=ALU.mult, op1=ALU.add).then_inc(ff_added[j], 1)
                if banks[-1] == E // 2 - 1:
                    dve.wait_ge(ff_added[-1], 2 * t + 2)
                    nc.vector.tensor_tensor(tile, tile, odd[:], ALU.add).then_inc(ff_sum, 1)

            with dve.Fori(0, Y1) as t:
                add_experts(t, range(E // 2))

            def maxima(nth, slot_gen, par, qt):
                if qt == 0 and slot_gen is not None:
                    dve.wait_ge(msplit, slot_gen)
                dve.wait_ge(max_ready[qt % 2], 4 * nth + qt // 2 + 1)
                b = MAX_BANK[qt % 2]
                nc.vector.tensor_reduce(negm[:, par, qt:qt + 1], ps[:, b:b + 2, :].rearrange("p b c -> p (b c)"),
                                        AX.X, ALU.max, negate=True).then_inc(max_done[qt % 2], 1)

            def max_transpose(nth, par, gen):
                dve.wait_ge(msplit, 4 * (nth + 1))
                dve.wait_ge(mrow_out[par], 16 * gen)
                nc.vector.transpose(mt32[:, par], mpart[:, par]).then_inc(mt_done, 1)

            o = ps[:, TR_BANK, :].rearrange("p (g c v) -> p g c v", g=4, c=4)

            def denominators(pair):
                dve.wait_ge(tr_done, pair + 1)
                nc.vector.reciprocal(rden[:], o[:, :, :, DH]).then_inc(rden_done, 1)

            def normalise(pair):
                dve.wait_ge(rden_done, pair + 1)
                dve.wait_ge(y_done, pair)
                nc.vector.tensor_tensor(att[:].rearrange("p (c g d) -> p g c d", c=4, g=4), o[:, :, :, 0:DH],
                                        rden[:].unsqueeze(3).to_broadcast([P, 4, 4, DH]), ALU.mult
                                        ).then_inc(norm_done, 1)

            def statistics(pair):
                dve.wait_ge(y_done, pair + 1)
                nc.vector.bn_stats(ystat[:, bass.ds(pair, 1), :].rearrange("p o s -> p (o s)"),
                                   xn[:, bass.ds(pair, 1), :].rearrange("p o d -> p (o d)")).then_inc(ystat_done, 1)

            def step(i, u, pair=None):
                n = SLOTS * i + u
                for qt in range(NKT):
                    maxima(n + 2, 4 * (n + 1), u % 2, qt)
                    if qt == 1:
                        max_transpose(n + 1, (u + 1) % 2, 2 * i + (u + 1) // 2)
                    if pair is not None and u % 2 == 0 and qt == 3:
                        denominators(pair)
                    if pair is not None and u % 2 == 0 and qt == 5:
                        normalise(pair)
                    if pair is not None and u % 2 == 1 and qt == 3:
                        statistics(pair)

            for n in range(2):
                for qt in range(NKT):
                    add_experts(Y1 + NKT // 2 * n + qt // 2, range(qt % 2 * 2, qt % 2 * 2 + 2))
                    if n == 1 and qt == NKT - 1:
                        dve.wait_ge(ff_added[-1], 2 * NT)
                        nc.vector.memset(ps[:, PV_BANK, 0:POS // 4], 0.0).then_inc(att_const, 1)
                    maxima(n, None, n, qt)
                    if n == 1 and qt == 1:
                        max_transpose(0, 0, 0)
            for u in range(SLOTS):
                step(0, u, pair=0 if u >= 2 else None)
            with dve.Fori(1, NB // SLOTS - 1) as i:
                for u in range(SLOTS):
                    step(i, u, pair=2 * i + u // 2 - 1)
            last = NB // SLOTS - 1
            for u in range(2):
                step(last, u, pair=2 * last - 1)

            def aggregate(part, entries):
                dve.wait_ge(ystat_done, TPB * entries.stop)
                for b in range(entries.start, entries.stop):
                    last_aggr = nc.vector.bn_aggr(bmv[:, b, :], ystat[:, b * TPB:(b + 1) * TPB, :].rearrange("p t s -> p (t s)"))
                last_aggr.then_inc(fin_d, 1)

            def deviations(part, entries):
                n = entries.stop - entries.start
                dve.wait_ge(fin_pe, 2 * part + 1)
                nc.vector.tensor_copy(bmean[:, entries], ps[:, 2 * part, 0:2 * n].rearrange("p (b s) -> p b s", s=2)
                                      ).then_inc(fin_d, 1)
                dve.wait_ge(fin_d, 7 * part + 2)
                nc.vector.tensor_tensor(dev2[:, entries], bmv[:, entries, 0], bmean[:, entries, 0],
                                        ALU.subtract).then_inc(fin_d, 1)
                dve.wait_ge(fin_d, 7 * part + 3)
                nc.vector.tensor_tensor(dev2[:, entries], dev2[:, entries], dev2[:, entries], ALU.mult).then_inc(fin_d, 1)

            def variances(part, entries):
                dve.wait_ge(fin_pe, 2 * part + 2)
                nc.vector.tensor_tensor(bvar[:, entries], bmean[:, entries, 1],
                                        ps[:, 2 * part + 1, 0:entries.stop - entries.start], ALU.add).then_inc(fin_d, 1)
                dve.wait_ge(fin_d, 7 * part + 5)
                nc.vector.tensor_scalar(bvar[:, entries], bvar[:, entries], EPS, None, ALU.add).then_inc(fin_d, 1)
                dve.wait_ge(fin_pool, part + 1)
                nc.vector.scalar_tensor_tensor(out=bshift[:, entries], in0=bmean[:, entries, 0], scalar=-1.0,
                                               in1=brstd[:, entries], op0=ALU.mult, op1=ALU.mult).then_inc(fin_d, 1)

            early, late = slice(0, EARLY), slice(EARLY, BATCH)
            aggregate(0, early)
            max_transpose(NB - 1, 1, NB // 2 - 1)
            deviations(0, early)
            denominators(NB // 2 - 2)
            normalise(NB // 2 - 2)
            variances(0, early)
            statistics(NB // 2 - 2)
            dve.wait_ge(ff_sum, NT)
            dve.wait_ge(fin_d, 7)
            for c in range(EARLY * NC // BATCH):
                p, b = c % 2, c * BATCH // NC
                if c >= 2:
                    dve.wait_ge(o_done, c - 1)
                nc.vector.tensor_scalar(xnc[:, p], xn[:, TC * c:TC * (c + 1), :], brstd[:, b:b + 1], bshift[:, b:b + 1],
                                        ALU.mult, ALU.add).then_inc(zd_done, 1)
                dve.wait_ge(zd_done, c + 1)
                if c >= 4:
                    dve.wait_ge(o_out[c % 4], 16)
                nc.vector.tensor_tensor(outs[c % 4], xnc[:, p], acc[:, TC * c:TC * (c + 1), :], ALU.add).then_inc(o_done, 1)

            denominators(NB // 2 - 1)
            normalise(NB // 2 - 1)
            statistics(NB // 2 - 1)
            aggregate(1, late)
            deviations(1, late)
            variances(1, late)
            for p in range(2):
                c = EARLY * NC // BATCH + p
                dve.wait_ge(o_out[c % 4], 16 * (c // 4))
                for h in range(2):
                    dve.wait_ge(z_done, 2 * p + h + 1)
                    t = slice(h * TC // 2, (h + 1) * TC // 2)
                    first_tile = EARLY * TPB + TC * p
                    nc.vector.tensor_tensor(outs[c % 4][:, t], xnc[:, p, t], acc[:, first_tile + t.start:first_tile + t.stop, :],
                                            ALU.add).then_inc(o_done, 1)

        @block.tensor
        def _(pe):
            def transposes(c, k, p):
                pe.wait_ge(xn_done, TC * (c + 1))
                pe.wait_ge(xtl_done, KT * c)
                for kt in range(KT):
                    for t in range(TC):
                        last = nc.tensor.transpose(ps[:, XT_BANK[kt], t * P:(t + 1) * P],
                                                   xnc[:, p, t, kt * P:(kt + 1) * P], ident[:])
                    last.then_inc(xt_psum[p], 1)

            def project_qk(c, p):
                pe.wait_ge(xtl_done, KT * (c + 1))
                for o in range(4):
                    pe.wait_ge(qk_evac, 4 * c + o - 1 if o > 1 else 4 * c)
                    products = [(w, v, kt) for w, v in ((wqkh, xth), (wqkh, xtl), (wqkl, xth)) for kt in range(KT)]
                    for i, (w, v, kt) in enumerate(products):
                        last = nc.tensor.matmul(ps[:, QK_BANK[o], :], w[:, o // 2, kt, (o % 2) * P:(o % 2 + 1) * P],
                                                v[:, p, kt, :], start=i == 0, stop=i == len(products) - 1)
                    last.then_inc(qk_ready, 1)

            def project_v(c, p, t):
                bank = V_BANK[t % 2]
                pe.wait_ge(v_evac[t % 2], 2 * c + t // 2)
                pe.wait_ge(lg_evac[t % 2], 2 * c + t // 2)
                products = [(x_t, w, kt) for kt in range(KT) for x_t, w in ((xth, wvgh), (xth, wvgl), (xtl, wvgh))]
                for i, (x_t, w, kt) in enumerate(products):
                    last = nc.tensor.matmul(ps[:, bank, 0:D + E], x_t[:, p, kt, t * P:(t + 1) * P], w[:, kt, :],
                                            start=i == 0, stop=i == len(products) - 1)
                last.then_inc(v_ready[t % 2], 1)

            def expert_product(e, s):
                if s == 0:
                    pe.wait_ge(ml_done, KT * e)
                pe.wait_ge(w_in_s[s], 32 * (e + 1))
                for dh in range(KT):
                    for h in range(HU):
                        last = nc.tensor.matmul(ps[:, M_BANK[dh], 0:D], win[s][:, h, dh * P:(dh + 1) * P],
                                                wout[s][:, h, :], start=s == 0 and h == 0,
                                                stop=s == 1 and h == HU - 1)
                    if s == 1:
                        last.then_inc(m_ready, 1)
                    elif dh == KT - 1:
                        last.then_inc(first_half, 1)

            def chunk(c, p, k_next=None):
                project_qk(c, p)
                project_v(c, p, 0)
                project_v(c, p, 1)
                if k_next is not None:
                    transposes(c + 1, k_next, 1 - p)
                project_v(c, p, 2)
                project_v(c, p, 3)
                if k_next is not None:
                    expert_product(c + 1, 0)
                    expert_product(c + 1, 1)

            expert_product(0, 0)
            pe.wait_ge(const_step, 6 + E)
            transposes(0, 0, 0)
            expert_product(0, 1)
            pe.wait_ge(w_lo, 2)
            with pe.Fori(0, NC // 2 - 1) as k:
                for p in range(2):
                    chunk(2 * k + p, p, k + p)
            chunk(NC - 2, 0, NC // 2 - 1)
            chunk(NC - 1, 1)

            def y_bank(t, slot, j):
                pe.wait_ge(ff_added[j], 2 * t)
                products = [(v, m, kt) for kt in range(KT) for v, m in ((xtth, mth), (xtth, mtl), (xttl, mth))]
                for i, (v, m, kt) in enumerate(products):
                    last = nc.tensor.matmul(ps[:, Y_BANK[j], :], v[:, slot, kt, :],
                                            m[:, kt, 2 * j:2 * j + 2, :].rearrange("p e d -> p (e d)"),
                                            start=i == 0, stop=i == len(products) - 1)
                last.then_inc(y_ready[j], 1)

            pe.wait_ge(ml_done, KT * E)
            for h in range(2):
                pe.wait_ge(v_evac[h], 2 * NC)
                pe.wait_ge(lg_evac[h], 2 * NC)
            with pe.Fori(0, Y1 // XS) as k:
                for slot in range(XS):
                    pe.wait_ge(xtt_in[slot], 32 * (k + 1))
                    for j in range(E // 2):
                        y_bank(XS * k + slot, slot, j)

            def max_scores(i, u, n, qt):
                if qt == 0:
                    pe.wait_ge(feat_in[u], 96 * (i + 1))
                pe.wait_ge(max_done[qt % 2], 4 * n + qt // 2)
                for h in range(2):
                    last = nc.tensor.matmul(ps[:, MAX_BANK[qt % 2] + h, :], qf[0:FR, u, qt * P:(qt + 1) * P],
                                            kf[0:FR, u, h * HALF:(h + 1) * HALF], start=True, stop=True)
                last.then_inc(max_ready[qt % 2], 1)

            def scores(i, u, n, kt):
                if kt == 0:
                    pe.wait_ge(mrow_in[u], 48 * (i + 1))
                for h in range(2):
                    pe.wait_ge(exp_done[h], NKT * n + kt)
                    nc.tensor.matmul(ps[:, ST_BANK[h], :], kf[0:SR, u, kt * P:(kt + 1) * P],
                                     qf[0:SR, u, h * HALF:(h + 1) * HALF], start=True, stop=True
                                     ).then_inc(st_ready[h], 1)

            def sum_values(n, par, gen, kt):
                if kt == 0:
                    pe.wait_ge(vb_in[par], 32 * (gen + 1))
                    pe.wait_ge(pv_evac, n)
                for h in range(2):
                    pe.wait_ge(exp_done[h], NKT * n + kt + 1)
                for j in range(4):
                    last = nc.tensor.matmul(ps[32 * j:32 * j + VW, PV_BANK, 0:POS // 4], vb[:, par, kt, :],
                                            wp[:, kt % 4, j * (POS // 4):(j + 1) * (POS // 4)],
                                            start=kt == 0, stop=kt == NKT - 1, tile_position=(0, 32 * j))
                last.then_inc(pv_done[kt % 4], 1)

            def to_token_rows(pair):
                pe.wait_ge(pv_evac, 2 * pair + 2)
                pe.wait_ge(norm_done, pair)
                for g in range(4):
                    last = nc.tensor.transpose(ps[:, TR_BANK, g * P:(g + 1) * P],
                                               ot[:, g].rearrange("p b t -> p (b t)"), ident[:])
                last.then_inc(tr_done, 1)

            def mean_over_partitions(part, entries, which):
                n = entries.stop - entries.start
                if which == 0:
                    pe.wait_ge(fin_d, 7 * part + 1)
                    nc.tensor.matmul(ps[:, 2 * part, 0:2 * n], onesm[:], bmv[:, entries, :].rearrange("p b s -> p (b s)"),
                                     start=True, stop=True).then_inc(fin_pe, 1)
                else:
                    pe.wait_ge(fin_d, 7 * part + 4)
                    nc.tensor.matmul(ps[:, 2 * part + 1, 0:n], onesm[:], dev2[:, entries], start=True, stop=True
                                     ).then_inc(fin_pe, 1)

            def step(i, u, pair=None, before=True, has_max=True):
                n = SLOTS * i + u
                for kt in range(0, NKT, 2):
                    scores(i, u, n, kt)
                    if has_max:
                        for t in (kt, kt + 1):
                            max_scores(i + (u + 2) // SLOTS, (u + 2) % SLOTS, n + 2, t)
                    late = not has_max and kt != 2
                    if not late:
                        scores(i, u, n, kt + 1)
                    if kt == 2 and not before:
                        pe.wait_ge(att_const, 3)
                    if u == 2 and not has_max and kt in (2, 6):
                        mean_over_partitions(0, slice(0, EARLY), kt // 6)
                    for t in (kt - 2, kt - 1):
                        if late and t == kt - 1:
                            scores(i, u, n, kt + 1)
                        if kt:
                            sum_values(n, u % 2, 2 * i + u // 2, t)
                        elif before:
                            sum_values(n - 1, (u - 1) % 2, 2 * i + (u - 1) // 2, NKT + t)
                    if kt == 2 and pair is not None:
                        to_token_rows(pair)

            pe.wait_ge(qk_evac, 4 * NC)
            pe.wait_ge(att_const, 2)
            for n in range(2):
                for qt in range(NKT):
                    t = Y1 + NKT // 2 * n + qt // 2
                    if qt % 2 == 0:
                        pe.wait_ge(xtt_in[t % XS], 32 * (t // XS + 1))
                    for j in range(qt % 2 * 2, qt % 2 * 2 + 2):
                        y_bank(t, t % XS, j)
                    max_scores(0, n, n, qt)
            for j in range(2):
                pe.wait_ge(ff_added[j], 2 * NT)
            for u in range(SLOTS):
                step(0, u, pair=0 if u == 2 else None, before=u > 0)
            with pe.Fori(1, NB // SLOTS - 1) as i:
                for u in range(SLOTS):
                    step(i, u, pair=2 * i + u // 2 - 1 if u % 2 == 0 else None)
            last_i = NB // SLOTS - 1
            for u in range(SLOTS):
                step(last_i, u, pair=2 * last_i + u // 2 - 1 if u % 2 == 0 else None, has_max=u < 2)
            for t in (NKT - 2, NKT - 1):
                sum_values(NB - 1, 1, NB // 2 - 1, t)
            to_token_rows(NB // 2 - 1)

            for which in range(2):
                mean_over_partitions(1, slice(EARLY, BATCH), which)


def build(nc, arrays, out_shape):
    args = [nc.dram_tensor(name, a.shape, mybir.dt.from_np(a.dtype), kind="ExternalInput").ap()
            for name, a in arrays.items()]
    result = nc.dram_tensor("result", out_shape, FP32, kind="ExternalOutput").ap()
    attention_and_experts(nc, *args, result)


def kernel(L0_attn_x, L0_attn_Wq, L0_attn_Wk, L0_attn_Wv, L0_ffn_w_gate, L0_ffn_w_in, L0_ffn_w_out):
    import numpy as np
    import concourse.bacc as bacc
    from concourse.bass_utils import run_bass_kernel_spmd

    def laid_out(a, axes=None):
        a = np.asarray(a)
        return np.ascontiguousarray(a if axes is None else np.transpose(a, axes))

    arrays = {
        "x": laid_out(L0_attn_x),
        "wq_t": laid_out(L0_attn_Wq, (1, 0)),
        "wk_t": laid_out(L0_attn_Wk, (1, 0)),
        "wv_t": laid_out(L0_attn_Wv, (1, 0)),
        "wg_t": laid_out(L0_ffn_w_gate, (1, 0)),
        "w_in": laid_out(L0_ffn_w_in),
        "w_out_t": laid_out(L0_ffn_w_out, (0, 2, 1)),
    }
    nc = bacc.Bacc("TRN2", target_bir_lowering=False, num_devices=1)
    build(nc, arrays, arrays["x"].shape)
    r = run_bass_kernel_spmd(nc, [arrays], core_ids=[0])
    return r.results[0]["result"]
```
